# Optimizing a Trainium2 kernel written in Bass

```python
import numpy as np
import jax
import jax.numpy as jnp

def _softmax(x, axis=-1):
    return jax.nn.softmax(x, axis=axis)

def _gelu(x):
    return jax.nn.gelu(x, approximate=True)

def _silu(x):
    return jax.nn.silu(x)

def _sigmoid(x):
    return jax.nn.sigmoid(x)

def _layernorm(x, axis=-1, eps=1e-05):
    m = jnp.mean(x, axis=axis, keepdims=True)
    v = jnp.var(x, axis=axis, keepdims=True)
    return (x - m) / jnp.sqrt(v + eps)

def _scatter_add(tgt, idx, src, axis=0):
    return tgt.at[idx].add(src)

def _segment_sum(src, seg, n):
    return jax.ops.segment_sum(src, seg, n)
kernel_name = 'mk_sandwich_d1_jaxref_r8_6ab9f4'

def setup_inputs(seed: int=0):
    np.random.seed(seed)
    _w = jnp.asarray

    def _L0_attn_setup():
        import jax, jax.numpy as jnp
        import numpy as np
        DIM = 128
        HEADS = 16
        HEAD_DIM = DIM // HEADS
        K = 13
        NS = K // 2
        SCALE = HEAD_DIM ** (-0.5)
        key = jax.random.key(seed)
        ks = jax.random.split(key, 5)
        B, L = (2, 512)
        x = jax.random.normal(ks[0], (B, L, DIM), jnp.float32)
        qkv_w = jax.random.normal(ks[1], (3 * DIM, DIM), jnp.float32) * 0.02
        qkv_b = jnp.zeros((3 * DIM,), jnp.float32)
        rpb = jax.random.normal(ks[2], (HEADS, 2 * K - 1), jnp.float32) * 0.02
        proj_w = jax.random.normal(ks[3], (DIM, DIM), jnp.float32) * 0.02
        proj_b = jnp.zeros((DIM,), jnp.float32)
        return dict(x=x, qkv_w=qkv_w, qkv_b=qkv_b, rpb=rpb, proj_w=proj_w, proj_b=proj_b)
    _L0_attn_in = _L0_attn_setup()

    def _L0_ffn_setup():
        import jax, jax.numpy as jnp
        import numpy as np
        E, D, TOP_K = (8, 128, 2)
        EPS_NORM, EPS_COS = (1e-12, 1e-08)

        def _l2norm(v, eps):
            return v / jnp.maximum(jnp.linalg.norm(v, axis=-1, keepdims=True), eps)

        def _mlp(x, gw, uw, dw):
            return jax.nn.silu(x @ gw.T) * (x @ uw.T) @ dw.T
        key = jax.random.key(seed)
        ks = jax.random.split(key, 12)
        B, S, H, F_ = (2, 256, 128, 256)
        G = E * D
        w = lambda k, shp: jax.random.normal(k, shp, dtype=jnp.float32) * 0.02
        return {'hidden_states': jax.random.normal(ks[0], (B, S, H), dtype=jnp.float32), 'gru_w_ih': w(ks[1], (3 * G, H)), 'gru_w_hh': w(ks[2], (3 * G, G)), 'expr_w': w(ks[3], (G, H)), 'ctx_w': w(ks[4], (G, H)), 'ctx_b': jnp.zeros((G,), dtype=jnp.float32), 'gate_w': w(ks[5], (E, F_, H)), 'up_w': w(ks[6], (E, F_, H)), 'down_w': w(ks[7], (E, H, F_)), 'shared_gate_w': w(ks[8], (F_, H)), 'shared_up_w': w(ks[9], (F_, H)), 'shared_down_w': w(ks[10], (H, F_))}
    _L0_ffn_in = _L0_ffn_setup()
    _d = {'L0_attn_x': _L0_attn_in['x'], 'L0_attn_qkv_w': _L0_attn_in['qkv_w'], 'L0_attn_qkv_b': _L0_attn_in['qkv_b'], 'L0_attn_rpb': _L0_attn_in['rpb'], 'L0_attn_proj_w': _L0_attn_in['proj_w'], 'L0_attn_proj_b': _L0_attn_in['proj_b'], 'L0_ffn_gru_w_ih': _L0_ffn_in['gru_w_ih'], 'L0_ffn_gru_w_hh': _L0_ffn_in['gru_w_hh'], 'L0_ffn_expr_w': _L0_ffn_in['expr_w'], 'L0_ffn_ctx_w': _L0_ffn_in['ctx_w'], 'L0_ffn_ctx_b': _L0_ffn_in['ctx_b'], 'L0_ffn_gate_w': _L0_ffn_in['gate_w'], 'L0_ffn_up_w': _L0_ffn_in['up_w'], 'L0_ffn_down_w': _L0_ffn_in['down_w'], 'L0_ffn_shared_gate_w': _L0_ffn_in['shared_gate_w'], 'L0_ffn_shared_up_w': _L0_ffn_in['shared_up_w'], 'L0_ffn_shared_down_w': _L0_ffn_in['shared_down_w']}
    _x0 = _d['L0_attn_x']
    _d['L0_attn_x'] = jax.random.normal(jax.random.fold_in(jax.random.key(seed), 1), (8, 512, 128), dtype=_x0.dtype)
    del _x0
    return _d

def reference(L0_attn_x, L0_attn_qkv_w, L0_attn_qkv_b, L0_attn_rpb, L0_attn_proj_w, L0_attn_proj_b, L0_ffn_gru_w_ih, L0_ffn_gru_w_hh, L0_ffn_expr_w, L0_ffn_ctx_w, L0_ffn_ctx_b, L0_ffn_gate_w, L0_ffn_up_w, L0_ffn_down_w, L0_ffn_shared_gate_w, L0_ffn_shared_up_w, L0_ffn_shared_down_w):

    def _L0_attn_ref(x, qkv_w, qkv_b, rpb, proj_w, proj_b):
        import jax, jax.numpy as jnp
        import numpy as np
        DIM = 128
        HEADS = 16
        HEAD_DIM = DIM // HEADS
        K = 13
        NS = K // 2
        SCALE = HEAD_DIM ** (-0.5)
        B, L, C = x.shape
        qkv = (x @ qkv_w.T + qkv_b).reshape(B, L, 3, HEADS, HEAD_DIM).transpose(2, 0, 3, 1, 4)
        q, k, v = (qkv[0] * SCALE, qkv[1], qkv[2])
        i = jnp.arange(L)
        ni = jnp.clip(i - NS, 0, L - K)
        pi = NS + jnp.where(i < NS, NS - i, 0) + jnp.where(i + NS >= L, L - i - 1 - NS, 0)
        j = jnp.arange(K)
        nbr = ni[:, None] + j[None, :]
        bidx = pi[:, None] + j[None, :]
        kg = k[:, :, nbr, :]
        vg = v[:, :, nbr, :]
        attn = jnp.einsum('bhld,bhlkd->bhlk', q, kg) + rpb[:, bidx][None]
        attn = jax.nn.softmax(attn, axis=-1)
        out = jnp.einsum('bhlk,bhlkd->bhld', attn, vg)
        out = out.transpose(0, 2, 1, 3).reshape(B, L, C)
        return out @ proj_w.T + proj_b

    def _L0_ffn_ref(hidden_states, gru_w_ih, gru_w_hh, expr_w, ctx_w, ctx_b, gate_w, up_w, down_w, shared_gate_w, shared_up_w, shared_down_w):
        import jax, jax.numpy as jnp
        import numpy as np
        E, D, TOP_K = (8, 128, 2)
        EPS_NORM, EPS_COS = (1e-12, 1e-08)

        def _l2norm(v, eps):
            return v / jnp.maximum(jnp.linalg.norm(v, axis=-1, keepdims=True), eps)

        def _mlp(x, gw, uw, dw):
            return jax.nn.silu(x @ gw.T) * (x @ uw.T) @ dw.T
        B, S, H = hidden_states.shape
        h0 = hidden_states.mean(axis=1) @ ctx_w.T + ctx_b
        xw = hidden_states @ gru_w_ih.T

        def step(h, xw_t):
            hw = h @ gru_w_hh.T
            xr, xz, xn = jnp.split(xw_t, 3, axis=-1)
            hr, hz, hnn = jnp.split(hw, 3, axis=-1)
            r = jax.nn.sigmoid(xr + hr)
            z = jax.nn.sigmoid(xz + hz)
            n = jnp.tanh(xn + r * hnn)
            h_new = (1.0 - z) * n + z * h
            return (h_new, h_new)
        _, hs = jax.lax.scan(step, h0, jnp.swapaxes(xw, 0, 1))
        routing = jnp.swapaxes(hs, 0, 1).reshape(B, S, E, D)
        routing = _l2norm(routing, EPS_NORM)
        expr = (hidden_states @ expr_w.T).reshape(B, S, E, D)
        gram = jnp.einsum('bsed,bsfd->bsef', routing, routing)
        diff = gram - jnp.eye(E, dtype=routing.dtype)
        diff_n = _l2norm(diff, EPS_NORM)
        penalty = jnp.mean(jnp.sum(diff_n ** 2, axis=(-2, -1)))
        num = jnp.sum(expr * routing, axis=-1)
        den = jnp.maximum(jnp.linalg.norm(expr, axis=-1), EPS_COS) * jnp.maximum(jnp.linalg.norm(routing, axis=-1), EPS_COS)
        cos_dist = 1.0 - num / den
        scores = (cos_dist * (1.0 + penalty)).reshape(B * S, E)
        top_v, top_i = jax.lax.top_k(scores, TOP_K)
        mult = jax.nn.softmax(top_v, axis=-1)
        onehot = jax.nn.one_hot(top_i, E, dtype=mult.dtype)
        cw = jnp.einsum('tk,tke->te', mult, onehot)
        xf = hidden_states.reshape(B * S, H)
        out = jnp.zeros_like(xf)
        for e in range(E):
            out = out + cw[:, e:e + 1] * _mlp(xf, gate_w[e], up_w[e], down_w[e])
        moe = out.reshape(B, S, H)
        shared = jax.lax.stop_gradient(_mlp(hidden_states, shared_gate_w, shared_up_w, shared_down_w))
        return moe + shared
    x = L0_attn_x
    x = x + _layernorm(_L0_attn_ref(_layernorm(x, axis=-1), L0_attn_qkv_w, L0_attn_qkv_b, L0_attn_rpb, L0_attn_proj_w, L0_attn_proj_b), axis=-1)
    x = x + _layernorm(_L0_ffn_ref(_layernorm(x, axis=-1), L0_ffn_gru_w_ih, L0_ffn_gru_w_hh, L0_ffn_expr_w, L0_ffn_ctx_w, L0_ffn_ctx_b, L0_ffn_gate_w, L0_ffn_up_w, L0_ffn_down_w, L0_ffn_shared_gate_w, L0_ffn_shared_up_w, L0_ffn_shared_down_w), axis=-1)
    return x

_drawn_inputs = setup_inputs


def setup_inputs(seed=0):
    import zlib

    import numpy as np

    out = dict(_drawn_inputs(seed))
    spreads = {'L0_attn_qkv_b': (0.0, 0.1), 'L0_attn_proj_b': (0.0, 0.1), 'L0_ffn_ctx_b': (0.0, 2.0)}
    factors = {'L0_attn_rpb': 6.176, 'L0_ffn_ctx_w': 13.885}
    for name, (base, spread) in spreads.items():
        noise = np.random.default_rng([zlib.crc32(name.encode()), seed]).standard_normal(out[name].shape)
        drawn = base * np.exp(spread * noise) if base else spread * noise
        out[name] = jnp.asarray(drawn.astype(out[name].dtype))
    for name, factor in factors.items():
        out[name] = (out[name] * factor).astype(out[name].dtype)
    return out
```

```python
from contextlib import ExitStack

import concourse.bass as bass
from concourse import mybir

F32 = mybir.dt.float32
F16 = mybir.dt.float16
BF16 = mybir.dt.bfloat16
U32 = mybir.dt.uint32
ALU = mybir.AluOpType
ACT = mybir.ActivationFunctionType
AX_X = mybir.AxisListType.X
RMAX = bass.bass_isa.ReduceOp.max
RADD = bass.bass_isa.ReduceOp.add

P = 128
BANK = 512


def sandwich(nc, x, qkv_w, qkv_b, rpb, proj_w, proj_b, w_ih, w_hh, expr_w, ctx_w, ctx_b,
             gate_w, up_w, down_w, sgate_w, sup_w, sdown_w, out):
    B, L, C = x.shape
    HEADS = rpb.shape[0]
    K = (rpb.shape[1] + 1) // 2
    NS = K // 2
    HD = C // HEADS
    QSCALE = float(HD) ** -0.5
    TOK = B * L
    TPS = L // P
    G = w_hh.shape[1]
    GM = G // P
    CH = GM
    NEXP = gate_w.shape[0]
    FF = gate_w.shape[1]
    FC = FF // P
    NE = NEXP + 1
    SP_T = P // B
    NT = TOK // P
    HALF = CH // 2
    WIN = K * HEADS
    EPS = 1e-5
    assert C == P and B * 4 == 32 and G == NEXP * P and GM == 8

    x2_dram = nc.dram_tensor("x2_scratch", (B, L, C), F32, kind="Internal").ap()
    hs_dram = nc.dram_tensor("hs_scratch", (L, P, CH * B), F32, kind="Internal").ap()

    ctx = ExitStack()
    with ctx:
        def sb(name, shape, dt=F32):
            return ctx.enter_context(nc.sbuf_tensor(name, shape, dt))

        def sem(name):
            return ctx.enter_context(nc.semaphore(name))

        psum = ctx.enter_context(nc.psum_tensor("psum", [P, 8, BANK], F32))

        room = sb("room", [P, GM * CH * 3 * P])
        taken = [0]

        def carve(*dims):
            n = 1
            for d in dims:
                n *= d
            a = room[:, taken[0]:taken[0] + n]
            taken[0] += n
            assert taken[0] <= GM * CH * 3 * P
            names = " ".join(f"d{i}" for i in range(len(dims)))
            return a if len(dims) == 1 else a.rearrange(
                f"p ({names}) -> p {names}", **{f"d{i}": d for i, d in enumerate(dims)})

        xs_room = sb("xs_room", [P, (L + 1) * 3 * B // 2])
        raw = [xs_room[:, i * 3 * G:(i + 1) * 3 * G] for i in range(2)]
        x_parts = xs_room[:, :].bitcast(BF16).rearrange("p (t k) -> p t k", k=3 * B)
        xn2T = sb("xn2T", [P, TOK])
        w_ih_s = sb("w_ih_s", [P, 2, 2, 4, 3, P], F16)
        w_hh_s = room[:, :].bitcast(F16).rearrange("p (s h k g r) -> p s h k g r", s=2, h=2, k=4 * CH, g=3)
        exprT = sb("exprT", [P, G])
        ctxT = sb("ctxT", [P, G])
        wqp = sb("wqp", [P, 4 * P])
        ident = sb("ident", [P, P])
        head_of = sb("head_of", [P, HEADS])
        spread = sb("spread", [P, P // HEADS, P])
        bias_win = sb("bias_win", [P, TPS, HEADS, K])
        proj_bias = sb("proj_bias", [P, C])
        qkv_bias = sb("qkv_bias", [P, 3])
        ctx_bias = sb("ctx_bias", [P, CH])
        eps = sb("eps", [P, 1])
        w_max = sb("w_max", [P, GM + 1])
        w_top = sb("w_top", [P, 1])
        w_all = sb("w_all", [P, 1])
        w_exp = sb("w_exp", [P, 1], U32)
        w_scale = sb("w_scale", [P, 1], U32)
        w_unscale = sb("w_unscale", [P, 1], U32)
        scale_f = w_scale[:, :].bitcast(F32)
        unscale_f = w_unscale[:, :].bitcast(F32)

        in_ready = sem("in_ready")
        zeroed = sem("zeroed")
        consts = sem("consts")
        raw_in = [sem("raw_in0"), sem("raw_in1")]
        raw_tr = sem("raw_tr")
        raw_out = sem("raw_out")
        x_all = carve(NT, C)

        small = [(0, [(qkv_w, 3), (proj_w, 1)], wqp), (1, [(ctx_w, 8)], ctxT), (0, [(expr_w, 8)], exprT)]
        with nc.Block() as block:
            @block.sync
            def _(sp):
                for n, (q, parts, _) in enumerate(small):
                    if n >= 2:
                        sp.wait_ge(raw_tr, n - 1)
                    at = 0
                    for w, m in parts:
                        sp.dma_start(raw[q][:, at * P:(at + m) * P].rearrange("p (m k) -> p m k", m=m),
                                     w.rearrange("(m p) k -> p m k", p=P)).then_inc(raw_in[q], 16)
                        at += m
                for b in range(B):
                    sp.dma_start(x_all[:, b * TPS:(b + 1) * TPS, :],
                                 x[b].rearrange("(t p) c -> p t c", p=P)).then_inc(in_ready, 16)
                sp.dma_start(proj_bias[:, :], bass.AP(tensor=proj_b.tensor, offset=0, ap=[[0, P], [1, C]])).then_inc(in_ready, 16)
                sp.dma_start(qkv_bias[:, :], qkv_b.rearrange("(n p) -> p n", p=P),
                             allow_slow_non_contiguous=True).then_inc(in_ready, 16)
                sp.dma_start(ctx_bias[:, :], ctx_b.rearrange("(c p) -> p c", p=P),
                             allow_slow_non_contiguous=True).then_inc(in_ready, 16)
                for t in range(TPS):
                    lo, hi = (NS if t == 0 else 0), (P - NS if t == TPS - 1 else P)
                    sp.dma_start(bias_win[lo:hi, t, :, :],
                                 bass.AP(tensor=rpb.tensor, offset=NS, ap=[[0, hi - lo], [2 * K - 1, HEADS], [1, K]])
                                 ).then_inc(in_ready, 16)
                for n in range(NS):
                    for row, t, col in ((n, 0, 2 * NS - n), (P - NS + n, TPS - 1, NS - 1 - n)):
                        sp.dma_start(bias_win[row:row + 1, t, :, :], rpb[:, col:col + K].unsqueeze(0)).then_inc(in_ready, 16)
                sp.wait_ge(in_ready, 16 * (3 + B + TPS + 2 * NS))

            @block.gpsimd
            def _(pool):
                nc.gpsimd.memset(ident[:, :], 0.0).then_inc(zeroed, 1)
                nc.gpsimd.memset(spread[:, :, :], 0.0).then_inc(zeroed, 1)
                nc.gpsimd.memset(head_of[:, :], 1.0).then_inc(zeroed, 1)
                nc.gpsimd.memset(eps[:, :], EPS)
                pool.wait_ge(zeroed, 3)
                nc.gpsimd.affine_select(out=ident[:, :], in_=ident[:, :], compare_op=ALU.not_equal, fill=1.0,
                                        base=0, pattern=[[-1, P]], channel_multiplier=1).then_inc(consts, 1)
                sv = spread[:, :, :].rearrange("p j (h d) -> p j h d", h=HEADS)
                nc.gpsimd.affine_select(out=sv, in_=sv, compare_op=ALU.not_equal, fill=1.0, base=0,
                                        pattern=[[-HEADS, P // HEADS], [-1, HEADS], [0, HD]],
                                        channel_multiplier=1).then_inc(consts, 1)
                nc.gpsimd.affine_select(out=head_of[:, :], in_=head_of[:, :], compare_op=ALU.is_ge, fill=0.0,
                                        base=0, pattern=[[-HD, HEADS]], channel_multiplier=1).then_inc(consts, 1)
                pool.wait_ge(consts, 3)
                nc.gpsimd.affine_select(out=head_of[:, :], in_=head_of[:, :], compare_op=ALU.is_ge, fill=0.0,
                                        base=HD - 1, pattern=[[HD, HEADS]], channel_multiplier=-1).then_inc(consts, 1)

            @block.tensor
            def _(pe):
                pe.wait_ge(consts, 1)
                landed = [0, 0]
                for n, (q, parts, _) in enumerate(small):
                    landed[q] += 16 * len(parts)
                    pe.wait_ge(raw_in[q], landed[q])
                    if n >= 2:
                        pe.wait_ge(raw_out, n - 1)
                    for m in range(sum(k for _, k in parts)):
                        last = nc.tensor.transpose(psum[:, 2 * q + m // 4, (m % 4) * P:(m % 4 + 1) * P],
                                                   raw[q][:, m * P:(m + 1) * P], ident[:, :])
                    last.then_inc(raw_tr, 1)

            @block.scalar
            def _(act):
                act.wait_ge(in_ready, 16 * (3 + B + TPS + 2 * NS))
                nc.scalar.mul(qkv_bias[:, 0:1], qkv_bias[:, 0:1], QSCALE)
                for n, (q, parts, dst) in enumerate(small):
                    act.wait_ge(raw_tr, n + 1)
                    for h in range(sum(k for _, k in parts) // 4):
                        last = nc.scalar.copy(dst[:, h * BANK:(h + 1) * BANK], psum[:, 2 * q + h, :])
                    last.then_inc(raw_out, 1)

        att_prod = carve(K, L)
        pv_prod = carve(K, L)
        xn = carve(TPS, C)
        xnT = carve(L)
        qT, kT, vT = carve(L), carve(L), carve(L)
        scores = carve(TPS, K, HEADS)
        probs = carve(TPS, K, HEADS)
        pT = [carve(L), carve(L)]
        att = carve(TPS, C)
        x2 = carve(TPS, C)
        stats = sb("stats", [P, TPS, 6])
        mv = sb("mv", [P, TPS, 2])
        std = sb("std", [P, TPS])
        rstd = sb("rstd", [P, TPS])
        top = sb("top", [P, TPS, HEADS])
        total = sb("total", [P, TPS, HEADS])

        def window_ops(j):
            def ends(a, shift):
                if shift is None:
                    return a.rearrange("p (s l) -> p s l", s=1)[:, :, 0:1], None
            mid = (lambda a: a[:, NS:L - NS], lambda a: a[:, j:j + L - 2 * NS])

            def tok_ends(a):
                w = a[:, 0:NS].unsqueeze(1)
                return bass.AP(tensor=w.tensor, offset=w.offset, ap=[w.ap[0], (L - NS, 2), (1, NS)])

            def key_ends(a):
                w = a[:, j:j + 1].unsqueeze(1)
                return bass.AP(tensor=w.tensor, offset=w.offset, ap=[w.ap[0], (L - K, 2), (0, NS)])
            return mid, (tok_ends, key_ends)

        pooled = [j for j in range(K) if j % 3 == 0]
        norm_var = sem("norm_var")
        norm_std = sem("norm_std")
        xn_done = sem("xn_done")
        xnT_ps = sem("xnT_ps")
        xnT_done = sem("xnT_done")
        qkv_ps = sem("qkv_ps")
        qkv_done = sem("qkv_done")
        qk_dve = sem("qk_dve")
        qk_pool = sem("qk_pool")
        score_ps = sem("score_ps")
        shifted = sem("shifted")
        exps = sem("exps")
        probs_done = sem("probs_done")
        pT_ps = sem("pT_ps")
        pT_done = sem("pT_done")
        spread_ps = sem("spread_ps")
        pv_done = sem("pv_done")
        proj_ps = sem("proj_ps")
        x2_done = sem("x2_done")
        x2_stored = sem("x2_stored")
        xn2_done = sem("xn2_done")
        xn2T_ps = sem("xn2T_ps")
        xn2T_done = sem("xn2T_done")
        score_v = psum[:, 4:6, :].rearrange("p a (t w) -> p (a t) w", t=2)[:, :, 0:WIN]

        def layer_norm(dve, src, dst, n):
            for t in range(TPS):
                nc.vector.bn_stats(stats[:, t, :], src(t))
            dve.drain()
            for t in range(TPS):
                last = nc.vector.bn_aggr(mv[:, t, :], stats[:, t, :])
            last.then_inc(norm_var, 1)
            dve.wait_ge(norm_std, n)
            nc.vector.reciprocal(rstd[:, :], std[:, :])
            dve.drain()
            for t in range(TPS):
                last = nc.vector.tensor_scalar(dst(t), src(t), mv[:, t, 0:1], rstd[:, t:t + 1],
                                               ALU.subtract, ALU.mult)
            return last

        with nc.Block() as block:
            @block.sync
            def _(sp):
                with sp.Fori(0, B) as b:
                    sp.wait_ge(x2_done, b + 1)
                    sp.dma_start(x2_dram[bass.ds(b, 1)].rearrange("b (t p) c -> p (b t) c", p=P), x2).then_inc(x2_stored, 16)

            @block.vector
            def _(dve):
                with dve.Fori(0, B) as b:
                    xb = x_all[:, bass.ds(b * TPS, TPS), :]
                    layer_norm(dve, lambda t: xb[:, t, :], lambda t: xn[:, t, :], 3 * b + 1).then_inc(xn_done, 1)
                    dve.wait_ge(qkv_done, 3 * b + 3)
                    for j in range(K):
                        if j not in pooled:
                            for q_of, k_of in window_ops(j):
                                last = nc.vector.tensor_tensor(q_of(att_prod[:, j, :]), q_of(qT), k_of(kT), ALU.mult)
                            last.then_inc(qk_dve, 1)
                    dve.wait_ge(score_ps, b + 1)
                    nc.vector.tensor_tensor(scores, score_v.rearrange("p t (k h) -> p t k h", h=HEADS),
                                            bias_win[:, :, :, :].rearrange("p t h k -> p t k h"), ALU.add)
                    dve.drain()
                    nc.vector.tensor_reduce(top[:, :, :], scores.rearrange("p t k h -> p t h k"), axis=AX_X, op=ALU.max)
                    dve.drain()
                    nc.vector.tensor_tensor(scores, scores, top[:, :, :].unsqueeze(2).to_broadcast([P, TPS, K, HEADS]),
                                            ALU.subtract).then_inc(shifted, 1)
                    dve.wait_ge(exps, b + 1)
                    nc.vector.tensor_reduce(total[:, :, :], probs.rearrange("p t k h -> p t h k"), axis=AX_X, op=ALU.add)
                    dve.drain()
                    nc.vector.reciprocal(total[:, :, :], total[:, :, :])
                    dve.drain()
                    nc.vector.tensor_tensor(probs, probs, total[:, :, :].unsqueeze(2).to_broadcast([P, TPS, K, HEADS]),
                                            ALU.mult).then_inc(probs_done, 1)
                    for j in range(K):
                        dve.wait_ge(spread_ps, K * b + j + 1)
                        for p_of, v_of in window_ops(j):
                            last = nc.vector.tensor_tensor(p_of(pv_prod[:, j, :]), p_of(psum[:, j % 4, :]), v_of(vT), ALU.mult)
                        last.then_inc(pv_done, 1)
                    dve.wait_ge(proj_ps, b + 1)
                    nc.vector.tensor_tensor(att, psum[:, 4, :].rearrange("p (t c) -> p t c", t=TPS),
                                            proj_bias[:, :].unsqueeze(1).to_broadcast([P, TPS, C]), ALU.add)
                    dve.drain()
                    layer_norm(dve, lambda t: att[:, t, :], lambda t: att[:, t, :], 3 * b + 2)
                    dve.drain()
                    nc.vector.tensor_tensor(x2, att, xb, ALU.add).then_inc(x2_done, 1)
                    dve.drain()
                    layer_norm(dve, lambda t: x2[:, t, :], lambda t: xn[:, t, :], 3 * b + 3).then_inc(xn2_done, 1)
                    dve.wait_ge(x2_stored, 16 * b + 16)
                    dve.wait_ge(xn2T_ps, b + 1)

            @block.gpsimd
            def _(pool):
                with pool.Fori(0, B) as b:
                    pool.wait_ge(qkv_done, 3 * b + 3)
                    for j in pooled:
                        for q_of, k_of in window_ops(j):
                            last = nc.gpsimd.tensor_tensor(q_of(att_prod[:, j, :]), q_of(qT), k_of(kT), ALU.mult)
                        last.then_inc(qk_pool, 1)

            @block.scalar
            def _(act):
                def roots(n):
                    act.wait_ge(norm_var, n)
                    nc.scalar.activation(std[:, :], mv[:, :, 1], ACT.Sqrt, bias=eps[:, 0:1]).then_inc(norm_std, 1)

                with act.Fori(0, B) as b:
                    roots(3 * b + 1)
                    act.wait_ge(xnT_ps, b + 1)
                    nc.scalar.copy(xnT, psum[:, 0, :]).then_inc(xnT_done, 1)
                    act.wait_ge(qkv_ps, b + 1)
                    for n, dst in enumerate((qT, kT, vT)):
                        nc.scalar.activation(dst, psum[:, 1 + n, :], ACT.Identity, scale=QSCALE if n == 0 else 1.0,
                                             bias=qkv_bias[:, n:n + 1]).then_inc(qkv_done, 1)
                    act.wait_ge(shifted, b + 1)
                    nc.scalar.activation(probs, scores, ACT.Exp).then_inc(exps, 1)
                    act.wait_ge(pT_ps, b + 1)
                    nc.scalar.copy(pT[0], psum[:, 6, :])
                    nc.scalar.copy(pT[1][0:WIN - P, :], psum[0:WIN - P, 7, :]).then_inc(pT_done, 1)
                    roots(3 * b + 2)
                    roots(3 * b + 3)
                    act.wait_ge(xn2T_ps, b + 1)
                    dst = xn2T[:, :].rearrange("p (t b) -> p t b", b=B)[:, :, bass.ds(b, 1)]
                    nc.scalar.copy(dst, psum[:, 5, :].unsqueeze(2)).then_inc(xn2T_done, 1)

            @block.tensor
            def _(pe):
                with pe.Fori(0, B) as b:
                    pe.wait_ge(xn_done, b + 1)
                    for t in range(TPS):
                        last = nc.tensor.transpose(psum[:, 0, t * P:(t + 1) * P], xn[:, t, :], ident[:, :])
                    last.then_inc(xnT_ps, 1)
                    pe.wait_ge(xnT_done, b + 1)
                    for n in range(3):
                        last = nc.tensor.matmul(psum[:, 1 + n, :], wqp[:, n * P:(n + 1) * P], xnT, start=True, stop=True)
                    last.then_inc(qkv_ps, 1)
                    nd, npool = 0, 0
                    for j in range(K):
                        if j in pooled:
                            npool += 1
                            pe.wait_ge(qk_pool, len(pooled) * b + npool)
                        else:
                            nd += 1
                            pe.wait_ge(qk_dve, (K - len(pooled)) * b + nd)
                        for t in range(TPS):
                            last = nc.tensor.matmul(score_v[:, t, j * HEADS:(j + 1) * HEADS],
                                                    att_prod[:, j, t * P:(t + 1) * P], head_of[:, :],
                                                    start=True, stop=True)
                    last.then_inc(score_ps, 1)
                    pe.wait_ge(probs_done, b + 1)
                    for t in range(TPS):
                        row = probs[:, t, :, :].rearrange("p k h -> p (k h)")
                        nc.tensor.transpose(psum[:, 6, t * P:(t + 1) * P], row[:, 0:P], ident[:, :])
                        last = nc.tensor.transpose(psum[0:WIN - P, 7, t * P:(t + 1) * P], row[:, P:WIN], ident[:, :])
                    last.then_inc(pT_ps, 1)
                    pe.wait_ge(pT_done, b + 1)

                    def project(j):
                        pe.wait_ge(pv_done, K * b + j + 1)
                        for t in range(TPS):
                            last = nc.tensor.matmul(psum[:, 4, t * P:(t + 1) * P], pv_prod[:, j, t * P:(t + 1) * P],
                                                    wqp[:, 3 * P:4 * P], start=(j == 0 and t == 0), stop=(j == K - 1),
                                                    skip_group_check=True)
                        return last

                    for j in range(K):
                        if j >= 4:
                            pe.wait_ge(pv_done, K * b + j - 3)
                        half, rows = (0, P) if j < P // HEADS else (1, WIN - P)
                        nc.tensor.matmul(psum[:, j % 4, :], spread[0:rows, j % (P // HEADS), :], pT[half][0:rows, :],
                                         start=True, stop=True).then_inc(spread_ps, 1)
                        if j >= 2:
                            project(j - 2)
                    project(K - 2)
                    project(K - 1).then_inc(proj_ps, 1)
                    pe.wait_ge(xn2_done, b + 1)
                    for t in range(TPS):
                        last = nc.tensor.transpose(psum[:, 5, t * P:(t + 1) * P], xn[:, t, :], ident[:, :])
                    last.then_inc(xn2T_ps, 1)
                    pe.wait_ge(xn2T_done, b + 1)

        max_in = [sem("max_in0"), sem("max_in1")]
        max_read = sem("max_read")
        top_row = sem("top_row")
        top_all = sem("top_all")
        hh_rows = w_hh.rearrange("(g m p) k -> m p g k", g=3, p=P)
        ih_rows = w_ih.rearrange("(gm p) k -> p gm k", p=P)
        with nc.Block() as block:
            @block.sync
            def _(sp):
                for g in range(3):
                    sp.dma_start(raw[0][:, g * G:(g + 1) * G].rearrange("p (m k) -> p m k", k=C),
                                 ih_rows[:, g * GM:(g + 1) * GM, :]).then_inc(max_in[0], 16)
                with sp.Fori(0, GM // 2) as i:
                    for q in range(2):
                        sp.wait_ge(max_read, 2 * i + 1)
                        sp.dma_start(raw[1 - q].rearrange("p (g k) -> p g k", g=3)[:, :, :],
                                     hh_rows[bass.ds(2 * i + q, 1)].rearrange("m p g k -> p (m g) k")
                                     ).then_inc(max_in[1 - q], 16)
                        if q == 0:
                            sp.wait_ge(max_read, 2 * i + 1)

            @block.vector
            def _(dve):
                dve.wait_ge(max_in[0], 48)
                nc.vector.tensor_reduce(w_max[:, GM:GM + 1], raw[0], axis=AX_X, op=ALU.max,
                                        apply_absolute_value=True).then_inc(max_read, 1)
                with dve.Fori(0, GM // 2) as i:
                    for q in range(2):
                        dve.wait_ge(max_in[1 - q], 16 * i + (16 if q == 0 else 64))
                        nc.vector.tensor_reduce(w_max[:, bass.ds(2 * i + q, 1)], raw[1 - q], axis=AX_X, op=ALU.max,
                                                apply_absolute_value=True).then_inc(max_read, 1)
                dve.drain()
                nc.vector.tensor_reduce(w_top[:, :], w_max[:, :], axis=AX_X, op=ALU.max).then_inc(top_row, 1)
                dve.wait_ge(top_all, 1)
                nc.vector.tensor_scalar(w_all[:, :], w_all[:, :], 2.0 ** -100, None, ALU.max)
                dve.drain()
                nc.vector.tensor_scalar(w_exp[:, :], w_all[:, :].bitcast(U32), 0x7F800000, None, ALU.bitwise_and)
                dve.drain()
                nc.vector.tensor_scalar(w_scale[:, :], w_exp[:, :], -1.0, float(268 << 23), ALU.mult, ALU.add)
                nc.vector.tensor_scalar(w_unscale[:, :], w_exp[:, :], float(14 << 23), None, ALU.subtract)

            @block.gpsimd
            def _(pool):
                pool.wait_ge(top_row, 1)
                nc.gpsimd.partition_all_reduce(w_all[:, :], w_top[:, :], P, RMAX).then_inc(top_all, 1)

        rec_in = [sem("rec_in0"), sem("rec_in1")]
        rec_tr = sem("rec_tr")
        rec_hi = sem("rec_hi")
        rec_lo = sem("rec_lo")
        PLACE = (1, 2, 0)
        with nc.Block() as block:
            @block.sync
            def _(sp):
                for g in range(3):
                    sp.dma_start(raw[1][:, g * G:(g + 1) * G].rearrange("p (m k) -> p m k", k=C),
                                 ih_rows[:, g * GM:(g + 1) * GM, :]).then_inc(rec_in[1], 16)
                with sp.Fori(0, GM // 2) as i:
                    for q in range(2):
                        sp.wait_ge(rec_tr, 6 * i + (1 if q == 0 else 3))
                        sp.dma_start(raw[q].rearrange("p (g k) -> p g k", g=3)[:, :, :],
                                     hh_rows[bass.ds(i + HALF * q, 1)].rearrange("m p g k -> p (m g) k")
                                     ).then_inc(rec_in[q], 16)

            def by_group(g, m):
                return psum[:, 2 * g + m // 4, :].rearrange("p (j c u) -> p c j u", j=4, u=32)[:, m % 4]

            def banks(g):
                return psum[:, 2 * g:2 * g + 2, :].rearrange("p a (c r) -> p (a c) r", r=P)

            def in_groups(g):
                return psum[:, 2 * g:2 * g + 2, :].rearrange("p a (k u) -> p (a k) u", u=32)

            def halves(g, h):
                return psum[:, 2 * g + h, :].rearrange("p (j r) -> p j r", j=4)

            @block.tensor
            def _(pe):
                pe.wait_ge(rec_in[1], 48)
                for g in range(3):
                    for m in range(GM):
                        last = nc.tensor.transpose(by_group(g, m), raw[1][:, (g * GM + m) * P:(g * GM + m + 1) * P], ident[:, :])
                    last.then_inc(rec_tr, 1)
                with pe.Fori(0, GM // 2) as i:
                    for q in range(2):
                        pe.wait_ge(rec_in[q], 16 * i + (16 if q == 0 else 64))
                        for g in range(3):
                            pe.wait_ge(rec_lo, 6 * i + 3 * q + g + 1)
                            for c in range(CH):
                                last = nc.tensor.transpose(banks(g)[:, c, :], raw[q][:, g * G + c * P:g * G + (c + 1) * P], ident[:, :])
                            last.then_inc(rec_tr, 1)

            @block.scalar
            def _(act):
                for g in range(3):
                    act.wait_ge(rec_tr, g + 1)
                    for h in range(2):
                        last = nc.scalar.activation(w_ih_s[:, 0, h, :, PLACE[g], :], halves(g, h), ACT.Copy, scale=scale_f[:, 0:1])
                    last.then_inc(rec_hi, 1)
                with act.Fori(0, GM // 2) as i:
                    for q in range(2):
                        for g in range(3):
                            act.wait_ge(rec_tr, 6 * i + 3 * q + g + 4)
                            nc.scalar.activation(w_hh_s[:, 0, q, :, g, bass.ds(i * 32, 32)],
                                                 in_groups(g), ACT.Copy, scale=scale_f[:, 0:1]).then_inc(rec_hi, 1)

            @block.vector
            def _(dve):
                for g in range(3):
                    dve.wait_ge(rec_hi, g + 1)
                    for h in range(2):
                        last = nc.vector.scalar_tensor_tensor(w_ih_s[:, 1, h, :, PLACE[g], :], halves(g, h), scale_f[:, 0:1],
                                                              w_ih_s[:, 0, h, :, PLACE[g], :], ALU.mult, ALU.subtract)
                    last.then_inc(rec_lo, 1)
                with dve.Fori(0, GM // 2) as i:
                    for q in range(2):
                        for g in range(3):
                            dve.wait_ge(rec_hi, 6 * i + 3 * q + g + 4)
                            hi, lo = (w_hh_s[:, s, q, :, g, bass.ds(i * 32, 32)] for s in range(2))
                            nc.vector.scalar_tensor_tensor(lo, in_groups(g), scale_f[:, 0:1], hi,
                                                           ALU.mult, ALU.subtract).then_inc(rec_lo, 1)

        HB = HALF * B
        h_parts = sb("h_parts", [P, 2, CH, 4 * B], BF16)
        x_now = sb("x_now", [P, 2, 4 * B], BF16)
        h_full = sb("h_full", [P, 2, CH * B])
        turned = sb("turned", [P, 2, BANK])
        gates = sb("gates", [P, 2, 4, HB])
        rz = sb("rz", [P, 2, 2, HB])
        pre_n = sb("pre_n", [P, 2, HB])
        n_act = sb("n_act", [P, 2, HB])
        keep = sb("keep", [P, 2, HB])
        fresh = sb("fresh", [P, 2, HB])
        rest = sb("rest", [P, 2, HB])
        x_mean = sb("x_mean", [P, B])
        x_rest = sb("x_rest", [P, TOK // 4])
        mean_done = sem("mean_done")
        h0_ps = sem("h0_ps")
        cleared = sem("cleared")
        h_ready = [sem("h_readyA"), sem("h_readyB")]
        x_staged = sem("x_staged")
        x_used = sem("x_used")
        bank_free = [sem("bank_freeA"), sem("bank_freeB")]
        gates_ps = [sem("gates_psA"), sem("gates_psB")]
        gates_in = [sem("gates_inA"), sem("gates_inB")]
        rz_done = [sem("rz_doneA"), sem("rz_doneB")]
        pre_done = [sem("pre_doneA"), sem("pre_doneB")]
        n_done = [sem("n_doneA"), sem("n_doneB")]
        keep_done = [sem("keep_doneA"), sem("keep_doneB")]
        hs_stored = [sem("hs_stored0"), sem("hs_stored1")]

        def split_state(dve, full, parts, n):
            def part(i):
                return parts[:, :, i * B:(i + 1) * B].rearrange("p c b -> p c b")
            f = full.rearrange("p (c b) -> p c b", b=B)
            r = rest[:, n, :].rearrange("p (c b) -> p c b", b=B)
            nc.vector.tensor_tensor(r, f, part(0), ALU.subtract)
            nc.vector.tensor_tensor(part(1), f, part(0), ALU.subtract)
            dve.drain()
            return nc.vector.tensor_tensor(part(2), r, part(1), ALU.subtract)

        with nc.Block() as block:
            @block.gpsimd
            def _(pool):
                nc.gpsimd.memset(h_parts[:, :, :, :], 0.0).then_inc(cleared, 1)
                nc.gpsimd.memset(x_now[:, :, :], 0.0)
                nc.gpsimd.memset(x_parts[:, L, :], 0.0)

            @block.vector
            def _(dve):
                nc.vector.tensor_reduce(x_mean[:, :], xn2T[:, :].rearrange("p (t b) -> p b t", b=B), axis=AX_X, op=ALU.add)
                dve.drain()
                nc.vector.tensor_scalar(x_mean[:, :], x_mean[:, :], 1.0 / L, None, ALU.mult).then_inc(mean_done, 1)
                for i in range(4):
                    n = L // 4
                    src = xn2T[:, i * n * B:(i + 1) * n * B].rearrange("p (t b) -> p t b", b=B)
                    left = x_rest[:, :].rearrange("p (t b) -> p t b", b=B)
                    part = [x_parts[:, i * n:(i + 1) * n, s * B:(s + 1) * B] for s in range(3)]
                    nc.vector.tensor_copy(part[0], src)
                    dve.drain()
                    nc.vector.tensor_tensor(left, src, part[0], ALU.subtract)
                    nc.vector.tensor_tensor(part[1], src, part[0], ALU.subtract)
                    dve.drain()
                    nc.vector.tensor_tensor(part[2], left, part[1], ALU.subtract)
                    dve.drain()
                dve.wait_ge(h0_ps, 1)
                dve.wait_ge(cleared, 1)
                nc.vector.tensor_tensor(h_full[:, 0, :].rearrange("p (c b) -> p c b", b=B),
                                        psum[:, 0, 0:CH * B].rearrange("p (c b) -> p c b", b=B),
                                        ctx_bias[:, :].unsqueeze(2).to_broadcast([P, CH, B]), ALU.add)
                dve.drain()
                for half in range(2):
                    cs = slice(half * HALF, (half + 1) * HALF)
                    full = h_full[:, 0, half * HB:(half + 1) * HB]
                    nc.vector.tensor_copy(h_parts[:, 0, cs, 0:B], full.rearrange("p (c b) -> p c b", b=B))
                    dve.drain()
                    split_state(dve, full, h_parts[:, 0, cs, :], half).then_inc(h_ready[half], 1)

            @block.tensor
            def _(pe):
                pe.wait_ge(mean_done, 1)
                for c in range(CH):
                    last = nc.tensor.matmul(psum[:, 0, c * B:(c + 1) * B], ctxT[:, c * P:(c + 1) * P], x_mean[:, :], start=True, stop=True)
                last.then_inc(h0_ps, 1)

        with nc.Block() as block:
            STEPS = 2

            @block.gpsimd
            def _(pool):
                pool.sem_inc(x_used, 2)
                pool.sem_inc(bank_free[0], 2)
                pool.sem_inc(bank_free[1], 2)
                pool.sem_inc(hs_stored[0], 16)
                pool.sem_inc(hs_stored[1], 16)
                nc.gpsimd.tensor_copy(x_now[:, 0, 0:3 * B], x_parts[:, 0, :]).then_inc(x_staged, 1)
                with pool.Fori(0, L // STEPS) as i:
                    t0 = i * STEPS
                    for q in range(STEPS):
                        pool.wait_ge(x_used, t0 + q + 2)
                        nc.gpsimd.tensor_copy(x_now[:, 1 - q, 0:3 * B].unsqueeze(1), x_parts[:, bass.ds(t0 + q + 1, 1), :]).then_inc(x_staged, 1)
                        for half in range(2):
                            pool.wait_ge(rz_done[half], t0 + q + 1)
                            nc.gpsimd.tensor_tensor(keep[:, half, :], rz[:, half, 1, :], h_full[:, q, half * HB:(half + 1) * HB], ALU.mult)
                            pool.drain()
                            nc.gpsimd.tensor_scalar(rz[:, half, 1, :], rz[:, half, 1, :], -1.0, 1.0, ALU.mult, ALU.add).then_inc(keep_done[half], 1)

            @block.tensor
            def _(pe):
                with pe.Fori(0, L // STEPS) as i:
                    t0 = i * STEPS
                    for q in range(STEPS):
                        pe.wait_ge(x_staged, t0 + q + 1)
                        for half in range(2):
                            pe.wait_ge(bank_free[half], t0 + q + 1)
                            for s in range(2):
                                for j in range(4):
                                    last = nc.tensor.matmul(psum[32 * j:32 * j + 32, 2 * q + half, 0:3 * P], x_now[:, q, :],
                                                            w_ih_s[:, s, half, j, :, :].rearrange("p g r -> p (g r)"),
                                                            start=(s == 0), stop=False, skip_group_check=True)
                        last.then_inc(x_used, 1)
                        for kh in range(2):
                            pe.wait_ge(h_ready[kh], t0 + q + 1)
                            for half in range(2):
                                for c in range(kh * HALF, (kh + 1) * HALF):
                                    for s in range(2):
                                        for j in range(4):
                                            last = nc.tensor.matmul(psum[32 * j:32 * j + 32, 2 * q + half, P:4 * P], h_parts[:, q, c, :],
                                                                    w_hh_s[:, s, half, 4 * c + j, :, :].rearrange("p g r -> p (g r)"),
                                                                    start=False, stop=(c == CH - 1 and s == 1), skip_group_check=True)
                                if kh == 1:
                                    last.then_inc(gates_ps[half], 1)

            @block.vector
            def _(dve):
                with dve.Fori(0, L // STEPS) as i:
                    t0 = i * STEPS
                    for q in range(STEPS):
                        t1 = t0 + q + 1
                        for half in range(2):
                            dve.wait_ge(gates_ps[half], t1)
                            nc.vector.transpose(turned[:, half, :], psum[:, 2 * q + half, :]).then_inc(bank_free[half], 1)
                            dve.drain()
                            nc.vector.tensor_reduce(gates[:, half, :, :].rearrange("p g (k b) -> p (g k) b", b=B),
                                                    turned[:, half, :].rearrange("p (k s b) -> p k b s", s=4, b=B)[:, :, :, 0:3],
                                                    axis=AX_X, op=ALU.add).then_inc(gates_in[half], 1)
                            dve.wait_ge(rz_done[half], t1)
                            nc.vector.tensor_tensor(pre_n[:, half, :], rz[:, half, 0, :], gates[:, half, 3, :], ALU.mult)
                            dve.drain()
                            nc.vector.tensor_tensor(pre_n[:, half, :], pre_n[:, half, :], gates[:, half, 0, :], ALU.add).then_inc(pre_done[half], 1)
                            dve.wait_ge(n_done[half], t1)
                            dve.wait_ge(keep_done[half], t1)
                            nc.vector.tensor_tensor(fresh[:, half, :], rz[:, half, 1, :], n_act[:, half, :], ALU.mult)
                            dve.drain()
                            if half == 0:
                                dve.wait_ge(hs_stored[q], 16 * i + 16)
                            full = h_full[:, 1 - q, half * HB:(half + 1) * HB]
                            parts = h_parts[:, 1 - q, half * HALF:(half + 1) * HALF, :]
                            nc.vector.tensor_tensor(full, fresh[:, half, :], keep[:, half, :], ALU.add)
                            nc.vector.tensor_tensor(parts[:, :, 0:B], fresh[:, half, :].rearrange("p (c b) -> p c b", b=B),
                                                    keep[:, half, :].rearrange("p (c b) -> p c b", b=B), ALU.add)
                            dve.drain()
                            split_state(dve, full, parts, half).then_inc(h_ready[half], 1)

            @block.scalar
            def _(act):
                with act.Fori(0, L // STEPS) as i:
                    t0 = i * STEPS
                    for q in range(STEPS):
                        t1 = t0 + q + 1
                        for half in range(2):
                            act.wait_ge(gates_in[half], t1)
                            nc.scalar.activation(rz[:, half, :, :], gates[:, half, 1:3, :], ACT.Sigmoid,
                                                 scale=unscale_f[:, 0:1]).then_inc(rz_done[half], 1)
                            act.wait_ge(pre_done[half], t1)
                            nc.scalar.activation(n_act[:, half, :], pre_n[:, half, :], ACT.Tanh,
                                                 scale=unscale_f[:, 0:1]).then_inc(n_done[half], 1)

            @block.sync
            def _(sp):
                with sp.Fori(0, L // STEPS) as i:
                    t0 = i * STEPS
                    for q in range(STEPS):
                        sp.wait_ge(h_ready[1], t0 + q + 2)
                        sp.dma_start(hs_dram[bass.ds(t0 + q, 1)].rearrange("t p k -> p (t k)"), h_full[:, 1 - q, :]).then_inc(hs_stored[q], 16)
                for q in range(STEPS):
                    sp.wait_ge(hs_stored[q], 16 * (L // STEPS + 1))

        taken[0] = 0
        expT = carve(NE, 6, P)
        gram = carve(NT, 7, NEXP)
        mix = carve(NT, NEXP)
        shared_room = taken[0]
        hst = [carve(SP_T, CH * B) for _ in range(2)]
        hst_c = [carve(CH, SP_T, B) for _ in range(2)]
        wrap = NEXP // 2
        routes = [carve(NEXP + wrap, P) for _ in range(2)]
        x_tile = [carve(P) for _ in range(2)]
        expr = [carve(NEXP, P) for _ in range(2)]
        dots = [carve(7, NEXP) for _ in range(2)]
        squares = carve(4, P)
        ew_in = [sem("ew_in0"), sem("ew_in1")]
        ew_tr = sem("ew_tr")
        ew_out = sem("ew_out")
        loads = []
        for kind, (w, sw) in enumerate(((gate_w, sgate_w), (up_w, sup_w), (down_w, sdown_w))):
            for lo in range(0, NEXP, 4):
                loads.append((kind, lo, 4, w[lo:lo + 4]))
            loads.append((kind, NEXP, 1, sw.unsqueeze(0)))

        def rows_of(kind, w):
            if kind < 2:
                return w.rearrange("e (f p) k -> p (e f) k", p=P)
            return w.rearrange("e p (f k) -> p (e f) k", k=P)

        with nc.Block() as block:
            @block.sync
            def _(sp):
                for n, (kind, lo, ne, w) in enumerate(loads):
                    if n >= 2:
                        sp.wait_ge(ew_tr, n - 1)
                    if kind < 2:
                        sp.dma_start(raw[n % 2][:, 0:2 * ne * P].rearrange("p (e k) -> p e k", k=P), rows_of(kind, w)).then_inc(ew_in[n % 2], 16)
                    else:
                        sp.dma_start(raw[n % 2][:, 0:2 * ne * P].rearrange("p (e k) -> p e k", k=FF), w.rearrange("e p k -> p e k")).then_inc(ew_in[n % 2], 16)

            @block.tensor
            def _(pe):
                for n, (kind, lo, ne, w) in enumerate(loads):
                    pe.wait_ge(ew_in[n % 2], 16 * (n // 2 + 1))
                    if n >= 2:
                        pe.wait_ge(ew_out, n - 1)
                    for m in range(2 * ne):
                        last = nc.tensor.transpose(psum[:, 2 * (n % 2) + m // 4, (m % 4) * P:(m % 4 + 1) * P],
                                                   raw[n % 2][:, m * P:(m + 1) * P], ident[:, :])
                    last.then_inc(ew_tr, 1)

            @block.scalar
            def _(act):
                for n, (kind, lo, ne, w) in enumerate(loads):
                    act.wait_ge(ew_tr, n + 1)
                    for h in range((ne + 1) // 2):
                        k = min(2, ne - 2 * h)
                        last = nc.scalar.copy(expT[:, lo + 2 * h:lo + 2 * h + k, 2 * kind:2 * kind + 2, :],
                                              psum[:, 2 * (n % 2) + h, 0:2 * k * P].rearrange("p (e f r) -> p e f r", e=k, f=2))
                    last.then_inc(ew_out, 1)

        hst_in = [sem("hst_in0"), sem("hst_in1")]
        tile_staged = sem("tile_staged")
        route_ps = sem("route_ps")
        expr_ps = sem("expr_ps")
        route_done = sem("route_done")
        sq_done = sem("sq_done")
        expr_done = sem("expr_done")
        dots_done = sem("dots_done")
        act_sq = sb("act_sq", [P, P])
        with nc.Block() as block:
            @block.sync
            def _(sp):
                sp.sem_inc(route_ps, 2)
                with sp.Fori(0, NT // 2) as i:
                    for q in range(2):
                        sp.wait_ge(route_ps, 2 * i + q + 1)
                        sp.dma_start(hst[q], hs_dram[bass.ds((2 * i + q) * SP_T, SP_T)].rearrange("t p k -> p t k")).then_inc(hst_in[q], 16)

            @block.gpsimd
            def _(pool):
                pool.sem_inc(expr_ps, 2)
                with pool.Fori(0, NT // 2) as i:
                    for q in range(2):
                        pool.wait_ge(expr_ps, 2 * i + q + 1)
                        pool.wait_ge(route_ps, 2 * i + q + 1)
                        pool.wait_ge(hst_in[q], 16 * i + 16)
                        nc.gpsimd.tensor_copy(x_tile[q], xn2T[:, bass.ds((2 * i + q) * P, P)])
                        nc.gpsimd.tensor_copy(hst_c[q], hst[q].rearrange("p t (c b) -> p c t b", b=B)).then_inc(tile_staged, 1)

            @block.tensor
            def _(pe):
                pe.sem_inc(dots_done, 2)
                pe.sem_inc(route_done, 2)
                pe.sem_inc(sq_done, 2)
                with pe.Fori(0, NT // 2) as i:
                    for q in range(2):
                        n = 2 * i + q + 1
                        pe.wait_ge(tile_staged, n)
                        pe.wait_ge(route_done, n)
                        for c in range(CH):
                            last = nc.tensor.transpose(psum[:, 4 * q + c // 4, (c % 4) * P:(c % 4 + 1) * P],
                                                       hst_c[q][:, c, :, :].rearrange("p t b -> p (t b)"), ident[:, :])
                        last.then_inc(route_ps, 1)
                        pe.wait_ge(dots_done, n)
                        pe.wait_ge(sq_done, n)
                        for h in range(2):
                            last = nc.tensor.matmul(psum[:, 4 * q + 2 + h, :], x_tile[q], exprT[:, h * BANK:(h + 1) * BANK],
                                                    start=True, stop=True)
                        last.then_inc(expr_ps, 1)

            @block.scalar
            def _(act):
                with act.Fori(0, NT // 2) as i:
                    for q in range(2):
                        n = 2 * i + q + 1
                        act.wait_ge(route_ps, n + 2)
                        act.wait_ge(dots_done, n)
                        for h in range(2):
                            nc.scalar.copy(routes[q][:, 4 * h:4 * h + 4, :], psum[:, 4 * q + h, :].rearrange("p (e d) -> p e d", e=4))
                        last = nc.scalar.copy(routes[q][:, NEXP:NEXP + wrap, :], psum[:, 4 * q, :].rearrange("p (e d) -> p e d", e=4))
                        last.then_inc(route_done, 1)
                        act.drain()
                        act.wait_ge(expr_ps, n + 2)
                        for h in range(2):
                            last = nc.scalar.copy(expr[q][:, 4 * h:4 * h + 4, :], psum[:, 4 * q + 2 + h, :].rearrange("p (e d) -> p e d", e=4))
                        last.then_inc(expr_done, 1)
                        act.drain()
                        for e in range(NEXP):
                            nc.scalar.activation(act_sq[:, :], routes[q][:, e, :], ACT.Square, accum_out=dots[q][:, 0, e:e + 1])
                            act.drain()
                            last = nc.scalar.activation(act_sq[:, :], expr[q][:, e, :], ACT.Square,
                                                        accum_out=dots[q][:, 6, e:e + 1])
                            act.drain()
                        last.then_inc(sq_done, 1)

            @block.vector
            def _(dve):
                with dve.Fori(0, NT // 2) as i:
                    for q in range(2):
                        n = 2 * i + q + 1
                        dve.wait_ge(route_done, n + 2)
                        dve.wait_ge(expr_done, n)
                        k = 0
                        for s in range(1, 6):
                            for e in range(NEXP if s != wrap else wrap):
                                other = routes[q][:, e + s, :] if s <= wrap else expr[q][:, e, :]
                                if k >= 4:
                                    dve.drain()
                                last = nc.vector.tensor_tensor_reduce(
                                    out=squares[:, k % 4, :], in0=routes[q][:, e, :], in1=other, scale=1.0, scalar=0.0,
                                    op0=ALU.mult, op1=ALU.add,
                                    accum_out=dots[q][:, s, e:e + 1])
                                k += 1
                        dve.drain()
                        dve.wait_ge(sq_done, n + 2)
                        nc.vector.tensor_copy(gram[:, bass.ds(2 * i + q, 1), :, :].rearrange("p a s e -> p (a s) e"), dots[q]).then_inc(dots_done, 1)

        def wide(name, n=NEXP):
            return carve(NT, n)
        length = wide("length")
        inv12 = wide("inv12", NEXP + wrap)
        e_len = wide("e_len")
        gsq = carve(NT, NEXP + wrap)
        row_sq = wide("row_sq")
        tmp = wide("tmp")
        tmp2 = wide("tmp2")
        score = wide("score")
        best = wide("best")
        best_at = carve(NT, NEXP).bitcast(U32)
        best_f = wide("best_f")
        places = carve(NEXP)
        pen = carve(4)
        pair = carve(NT, 4)
        r1 = sem("lengths_sq")
        r2 = sem("lengths_rt")
        r3 = sem("row_sum")
        r4 = sem("row_root")
        r5 = sem("pen_part")
        r6 = sem("pen_sum")
        r7 = sem("places_set")
        r8 = sem("gap_done")
        r9 = sem("gap_exp")
        with nc.Block() as block:
            @block.scalar
            def _(act):
                nc.scalar.activation(length, gram[:, :, 0, :], ACT.Sqrt)
                nc.scalar.activation(e_len, gram[:, :, 6, :], ACT.Sqrt).then_inc(r2, 1)
                act.wait_ge(r3, 1)
                nc.scalar.activation(tmp, row_sq, ACT.Sqrt).then_inc(r4, 1)
                act.wait_ge(r8, 1)
                nc.scalar.activation(pair[:, :, 1:2], pair[:, :, 0:1], ACT.Exp).then_inc(r9, 1)

            @block.gpsimd
            def _(pool):
                nc.gpsimd.iota(places, pattern=[[1, NEXP]], base=0, channel_multiplier=0, allow_small_or_imprecise_dtypes=True).then_inc(r7, 1)
                pool.wait_ge(r5, 1)
                nc.gpsimd.partition_all_reduce(pen[:, 1:2], pen[:, 0:1], P, RADD).then_inc(r6, 1)

            @block.vector
            def _(dve):
                v = nc.vector

                def tt(o, a, b_, op):
                    r = v.tensor_tensor(o, a, b_, op)
                    dve.drain()
                    return r

                def ts(o, a, s1, s2, op0, op1=None):
                    r = v.tensor_scalar(o, a, s1, s2, op0, op1) if op1 is not None else v.tensor_scalar(o, a, s1, s2, op0)
                    dve.drain()
                    return r

                dve.wait_ge(r2, 1)
                inv = inv12[:, :, 0:NEXP]
                ts(inv, length, 1e-12, None, ALU.max)
                v.reciprocal(inv, inv)
                dve.drain()
                v.tensor_copy(inv12[:, :, NEXP:], inv12[:, :, 0:wrap])
                dve.drain()
                tt(tmp, gram[:, :, 0, :], inv, ALU.mult)
                tt(tmp, tmp, inv, ALU.mult)
                ts(tmp, tmp, 1.0, None, ALU.subtract)
                tt(row_sq, tmp, tmp, ALU.mult)
                for s in range(1, wrap + 1):
                    n = NEXP if s < wrap else wrap
                    g = gsq[:, :, wrap:wrap + n]
                    tt(g, gram[:, :, s, 0:n], inv12[:, :, 0:n], ALU.mult)
                    tt(g, g, inv12[:, :, s:s + n], ALU.mult)
                    tt(g, g, g, ALU.mult)
                    tt(row_sq[:, :, 0:n], row_sq[:, :, 0:n], g, ALU.add)
                    first = min(n, NEXP - s)
                    tt(row_sq[:, :, s:s + first], row_sq[:, :, s:s + first], g[:, :, 0:first], ALU.add)
                    if first < n:
                        tt(row_sq[:, :, 0:n - first], row_sq[:, :, 0:n - first], g[:, :, first:n], ALU.add)
                dve.drain().then_inc(r3, 1)
                dve.wait_ge(r4, 1)
                ts(tmp, tmp, 1e-12, None, ALU.max)
                v.reciprocal(tmp, tmp)
                dve.drain()
                tt(tmp2, row_sq, tmp, ALU.mult)
                tt(tmp2, tmp2, tmp, ALU.mult)
                v.tensor_reduce(pen[:, 0:1], tmp2.rearrange("p t e -> p (t e)"), axis=AX_X, op=ALU.add).then_inc(r5, 1)
                dve.drain()
                tt(tmp2, length, inv, ALU.mult)
                ts(tmp2, tmp2, 1e-8, None, ALU.max)
                ts(tmp, e_len, 1e-8, None, ALU.max)
                tt(tmp, tmp, tmp2, ALU.mult)
                v.reciprocal(tmp, tmp)
                dve.drain()
                tt(score, gram[:, :, 5, :], inv, ALU.mult)
                tt(score, score, tmp, ALU.mult)
                ts(score, score, -1.0, 1.0, ALU.mult, ALU.add)
                dve.wait_ge(r6, 1)
                ts(pen[:, 2:3], pen[:, 1:2], 1.0 / TOK, 1.0, ALU.mult, ALU.add)
                ts(score, score, pen[:, 2:3], None, ALU.mult)
                for n in range(NT):
                    v.max(best[:, n, :], score[:, n, :])
                dve.drain()
                for n in range(NT):
                    v.max_index(best_at[:, n, :], best[:, n, :], score[:, n, :])
                dve.drain()
                v.tensor_copy(best_f, best_at)
                tt(pair[:, :, 0:1], best[:, :, 1:2], best[:, :, 0:1], ALU.subtract)
                dve.drain().then_inc(r8, 1)
                dve.wait_ge(r9, 1)
                dve.wait_ge(r7, 1)
                ts(pair[:, :, 2:3], pair[:, :, 1:2], 1.0, None, ALU.add)
                v.reciprocal(pair[:, :, 2:3], pair[:, :, 2:3])
                dve.drain()
                tt(pair[:, :, 3:4], pair[:, :, 1:2], pair[:, :, 2:3], ALU.mult)
                every = places.unsqueeze(1).to_broadcast([P, NT, NEXP])
                tt(tmp, every, best_f[:, :, 0:1].to_broadcast([P, NT, NEXP]), ALU.is_equal)
                tt(mix, tmp, pair[:, :, 2:3].to_broadcast([P, NT, NEXP]), ALU.mult)
                tt(tmp, every, best_f[:, :, 1:2].to_broadcast([P, NT, NEXP]), ALU.is_equal)
                tt(tmp, tmp, pair[:, :, 3:4].to_broadcast([P, NT, NEXP]), ALU.mult)
                tt(mix, mix, tmp, ALU.add)

        QT = BANK // P
        taken[0] = shared_room
        hid_a = [carve(FC, BANK) for _ in range(2)]
        hid = [carve(FC, BANK) for _ in range(2)]
        acc = carve(QT, C)
        x2_in = carve(QT, C)
        y_out = carve(QT, C)
        x2t_in = sem("x2t_in")
        gate_ps = sem("gate_ps")
        silu_done = sem("silu_done")
        hid_done = sem("hid_done")
        down_ps = sem("down_ps")
        down_read = sem("down_read")
        f_var = sem("f_var")
        f_std = sem("f_std")
        y_done = sem("y_done")
        y_stored = sem("y_stored")

        def token_rows(dram, tile):
            return dram.rearrange("b t c -> t b c")[bass.ds(tile * SP_T, SP_T)]

        with nc.Block() as block:
            @block.sync
            def _(sp):
                sp.sem_inc(y_done, 1)
                with sp.Fori(0, NT // QT) as i:
                    sp.wait_ge(y_done, i + 1)
                    for t in range(QT):
                        sp.dma_start(x2_in[:, t, :], token_rows(x2_dram, i * QT + t)).then_inc(x2t_in, 16)
                    sp.wait_ge(y_done, i + 2)
                    for t in range(QT):
                        sp.dma_start(token_rows(out, i * QT + t), y_out[:, t, :]).then_inc(y_stored, 16)
                sp.wait_ge(y_stored, 16 * NT)

            @block.tensor
            def _(pe):
                pe.sem_inc(hid_done, 1)
                pe.sem_inc(down_read, 1)
                with pe.Fori(0, NT // QT) as i:
                    toks = xn2T[:, bass.ds(i * BANK, BANK)]

                    def down(e):
                        pe.wait_ge(hid_done, NE * i + e + 2)
                        pe.wait_ge(down_read, NE * i + e + 1)
                        for t in range(QT):
                            for f in range(FC):
                                last = nc.tensor.matmul(psum[:, 4 + e % 2, t * P:(t + 1) * P], hid[e % 2][:, f, t * P:(t + 1) * P],
                                                        expT[:, e, 4 + f, :], start=(f == 0), stop=(f == FC - 1))
                        last.then_inc(down_ps, 1)

                    for e in range(NE):
                        pe.wait_ge(hid_done, NE * i + e + 1)
                        for k in range(4):
                            last = nc.tensor.matmul(psum[:, k, :], expT[:, e, k, :], toks, start=True, stop=True)
                        last.then_inc(gate_ps, 1)
                        if e >= 1:
                            down(e - 1)
                    down(NE - 1)

            @block.scalar
            def _(act):
                with act.Fori(0, NT // QT) as i:
                    for e in range(NE):
                        act.wait_ge(gate_ps, NE * i + e + 1)
                        nc.scalar.activation(hid_a[e % 2], psum[:, 0:FC, :], ACT.Silu).then_inc(silu_done, 1)
                    act.wait_ge(f_var, i + 1)
                    nc.scalar.activation(std[:, :], mv[:, :, 1], ACT.Sqrt, bias=eps[:, 0:1]).then_inc(f_std, 1)

            @block.vector
            def _(dve):
                with dve.Fori(0, NT // QT) as i:
                    def collect(e):
                        dve.wait_ge(down_ps, NE * i + e + 1)
                        for t in range(QT):
                            y = psum[:, 4 + e % 2, t * P:(t + 1) * P]
                            if e == 0:
                                w = mix[:, bass.ds(i * QT + t, 1), e:e + 1].rearrange("p a b -> p (a b)")
                                last = nc.vector.tensor_scalar(acc[:, t, :], y, w, None, ALU.mult)
                            elif e < NEXP:
                                w = mix[:, bass.ds(i * QT + t, 1), e:e + 1].rearrange("p a b -> p (a b)")
                                last = nc.vector.scalar_tensor_tensor(acc[:, t, :], y, w, acc[:, t, :], ALU.mult, ALU.add)
                            else:
                                last = nc.vector.tensor_tensor(acc[:, t, :], y, acc[:, t, :], ALU.add)
                        last.then_inc(down_read, 1)
                        dve.drain()

                    for e in range(NE):
                        dve.wait_ge(silu_done, NE * i + e + 1)
                        nc.vector.tensor_tensor(hid[e % 2], hid_a[e % 2], psum[:, FC:2 * FC, :], ALU.mult).then_inc(hid_done, 1)
                        if e >= 1:
                            collect(e - 1)
                    collect(NE - 1)
                    for t in range(QT):
                        nc.vector.bn_stats(stats[:, t, :], acc[:, t, :])
                    dve.drain()
                    for t in range(QT):
                        last = nc.vector.bn_aggr(mv[:, t, :], stats[:, t, :])
                    last.then_inc(f_var, 1)
                    dve.wait_ge(f_std, i + 1)
                    nc.vector.reciprocal(rstd[:, :], std[:, :])
                    dve.drain()
                    for t in range(QT):
                        nc.vector.tensor_scalar(acc[:, t, :], acc[:, t, :], mv[:, t, 0:1], rstd[:, t:t + 1], ALU.subtract, ALU.mult)
                    dve.drain()
                    dve.wait_ge(x2t_in, 16 * QT * i + 16 * QT)
                    dve.wait_ge(y_stored, 16 * QT * i + 0) if False else None
                    nc.vector.tensor_tensor(y_out, acc, x2_in, ALU.add).then_inc(y_done, 1)
                    dve.wait_ge(y_stored, 16 * QT * i + 16 * QT)


_INS = ['L0_attn_x', 'L0_attn_qkv_w', 'L0_attn_qkv_b', 'L0_attn_rpb', 'L0_attn_proj_w', 'L0_attn_proj_b',
        'L0_ffn_gru_w_ih', 'L0_ffn_gru_w_hh', 'L0_ffn_expr_w', 'L0_ffn_ctx_w', 'L0_ffn_ctx_b', 'L0_ffn_gate_w',
        'L0_ffn_up_w', 'L0_ffn_down_w', 'L0_ffn_shared_gate_w', 'L0_ffn_shared_up_w', 'L0_ffn_shared_down_w']
_OUTS = [((8, 512, 128), 'float32')]


def kernel(**inputs):
    import numpy as _np
    import concourse.bacc as _bacc
    from concourse import mybir as _mybir
    from concourse.bass_utils import run_bass_kernel_spmd as _run

    nc = _bacc.Bacc("TRN2", target_bir_lowering=False, num_devices=1)
    arrays, args = {}, []
    for name in _INS:
        a = _np.ascontiguousarray(inputs[name])
        arrays[f"in_{name}_dram"] = a
        args.append(nc.dram_tensor(f"in_{name}_dram", a.shape, _mybir.dt.from_np(a.dtype), kind="ExternalInput").ap())
    for i, (shape, dtype) in enumerate(_OUTS):
        dt = _mybir.dt.from_np(_np.dtype(dtype))
        args.append(nc.dram_tensor(f"out_{i}_dram", shape, dt, kind="ExternalOutput").ap())
    sandwich(nc, *args)
    r = _run(nc, [arrays], core_ids=[0])
    got = tuple(r.results[0][f"out_{i}_dram"] for i in range(len(_OUTS)))
    return got[0]
```

```python
from contextlib import ExitStack

import concourse.bass as bass
from concourse import mybir

F32 = mybir.dt.float32
F16 = mybir.dt.float16
BF16 = mybir.dt.bfloat16
U32 = mybir.dt.uint32
ALU = mybir.AluOpType
ACT = mybir.ActivationFunctionType
AX_X = mybir.AxisListType.X
RMAX = bass.bass_isa.ReduceOp.max
RADD = bass.bass_isa.ReduceOp.add

P = 128
BANK = 512


def sandwich(nc, x, qkv_w, qkv_b, rpb, proj_w, proj_b, w_ih, w_hh, expr_w, ctx_w, ctx_b,
             gate_w, up_w, down_w, sgate_w, sup_w, sdown_w, out):
    B, L, C = x.shape
    HEADS = rpb.shape[0]
    K = (rpb.shape[1] + 1) // 2
    NS = K // 2
    HD = C // HEADS
    QSCALE = float(HD) ** -0.5
    TOK = B * L
    TPS = L // P
    G = w_hh.shape[1]
    GM = G // P
    CH = GM
    NEXP = gate_w.shape[0]
    FF = gate_w.shape[1]
    FC = FF // P
    NE = NEXP + 1
    SP_T = P // B
    NT = TOK // P
    HALF = CH // 2
    WIN = K * HEADS
    EPS = 1e-5
    assert C == P and B * 4 == 32 and G == NEXP * P and GM == 8

    x2_dram = nc.dram_tensor("x2_scratch", (B, L, C), F32, kind="Internal").ap()
    hs_dram = nc.dram_tensor("hs_scratch", (L, P, CH * B), F32, kind="Internal").ap()

    ctx = ExitStack()
    with ctx:
        def sb(name, shape, dt=F32):
            return ctx.enter_context(nc.sbuf_tensor(name, shape, dt))

        def sem(name):
            return ctx.enter_context(nc.semaphore(name))

        psum = ctx.enter_context(nc.psum_tensor("psum", [P, 8, BANK], F32))

        room = sb("room", [P, GM * CH * 3 * P])
        taken = [0]

        def carve(*dims):
            n = 1
            for d in dims:
                n *= d
            a = room[:, taken[0]:taken[0] + n]
            taken[0] += n
            assert taken[0] <= GM * CH * 3 * P
            names = " ".join(f"d{i}" for i in range(len(dims)))
            return a if len(dims) == 1 else a.rearrange(
                f"p ({names}) -> p {names}", **{f"d{i}": d for i, d in enumerate(dims)})

        xs_room = sb("xs_room", [P, (L + 1) * 3 * B // 2])
        raw = [xs_room[:, i * 3 * G:(i + 1) * 3 * G] for i in range(2)]
        x_parts = xs_room[:, :].bitcast(BF16).rearrange("p (t k) -> p t k", k=3 * B)
        xn2T = sb("xn2T", [P, TOK])
        w_ih_s = sb("w_ih_s", [P, 2, 2, 4, 3, P], F16)
        w_hh_s = room[:, :].bitcast(F16).rearrange("p (s h k g r) -> p s h k g r", s=2, h=2, k=4 * CH, g=3)
        exprT = sb("exprT", [P, G])
        ctxT = sb("ctxT", [P, G])
        wqp = sb("wqp", [P, 4 * P])
        ident = sb("ident", [P, P])
        head_of = sb("head_of", [P, HEADS])
        spread = sb("spread", [P, P // HEADS, P])
        bias_win = sb("bias_win", [P, TPS, HEADS, K])
        proj_bias = sb("proj_bias", [P, C])
        qkv_bias = sb("qkv_bias", [P, 3])
        ctx_bias = sb("ctx_bias", [P, CH])
        eps = sb("eps", [P, 1])
        w_max = sb("w_max", [P, GM + 1])
        w_top = sb("w_top", [P, 1])
        w_all = sb("w_all", [P, 1])
        w_exp = sb("w_exp", [P, 1], U32)
        w_scale = sb("w_scale", [P, 1], U32)
        w_unscale = sb("w_unscale", [P, 1], U32)
        scale_f = w_scale[:, :].bitcast(F32)
        unscale_f = w_unscale[:, :].bitcast(F32)

        in_ready = sem("in_ready")
        zeroed = sem("zeroed")
        consts = sem("consts")
        raw_in = [sem("raw_in0"), sem("raw_in1")]
        raw_tr = sem("raw_tr")
        raw_out = sem("raw_out")
        x_all = carve(NT, C)

        small = [(0, [(qkv_w, 3), (proj_w, 1)], wqp), (1, [(ctx_w, 8)], ctxT), (0, [(expr_w, 8)], exprT)]
        with nc.Block() as block:
            @block.sync
            def _(sp):
                for n, (q, parts, _) in enumerate(small):
                    if n >= 2:
                        sp.wait_ge(raw_tr, n - 1)
                    at = 0
                    for w, m in parts:
                        sp.dma_start(raw[q][:, at * P:(at + m) * P].rearrange("p (m k) -> p m k", m=m),
                                     w.rearrange("(m p) k -> p m k", p=P)).then_inc(raw_in[q], 16)
                        at += m
                for b in range(B):
                    sp.dma_start(x_all[:, b * TPS:(b + 1) * TPS, :],
                                 x[b].rearrange("(t p) c -> p t c", p=P)).then_inc(in_ready, 16)
                sp.dma_start(proj_bias[:, :], bass.AP(tensor=proj_b.tensor, offset=0, ap=[[0, P], [1, C]])).then_inc(in_ready, 16)
                sp.dma_start(qkv_bias[:, :], qkv_b.rearrange("(n p) -> p n", p=P),
                             allow_slow_non_contiguous=True).then_inc(in_ready, 16)
                sp.dma_start(ctx_bias[:, :], ctx_b.rearrange("(c p) -> p c", p=P),
                             allow_slow_non_contiguous=True).then_inc(in_ready, 16)
                for t in range(TPS):
                    lo, hi = (NS if t == 0 else 0), (P - NS if t == TPS - 1 else P)
                    sp.dma_start(bias_win[lo:hi, t, :, :],
                                 bass.AP(tensor=rpb.tensor, offset=NS, ap=[[0, hi - lo], [2 * K - 1, HEADS], [1, K]])
                                 ).then_inc(in_ready, 16)
                for n in range(NS):
                    for row, t, col in ((n, 0, 2 * NS - n), (P - NS + n, TPS - 1, NS - 1 - n)):
                        sp.dma_start(bias_win[row:row + 1, t, :, :], rpb[:, col:col + K].unsqueeze(0)).then_inc(in_ready, 16)
                sp.wait_ge(in_ready, 16 * (3 + B + TPS + 2 * NS))

            @block.gpsimd
            def _(pool):
                nc.gpsimd.memset(ident[:, :], 0.0).then_inc(zeroed, 1)
                nc.gpsimd.memset(spread[:, :, :], 0.0).then_inc(zeroed, 1)
                nc.gpsimd.memset(head_of[:, :], 1.0).then_inc(zeroed, 1)
                nc.gpsimd.memset(eps[:, :], EPS)
                pool.wait_ge(zeroed, 3)
                nc.gpsimd.affine_select(out=ident[:, :], in_=ident[:, :], compare_op=ALU.not_equal, fill=1.0,
                                        base=0, pattern=[[-1, P]], channel_multiplier=1).then_inc(consts, 1)
                sv = spread[:, :, :].rearrange("p j (h d) -> p j h d", h=HEADS)
                nc.gpsimd.affine_select(out=sv, in_=sv, compare_op=ALU.not_equal, fill=1.0, base=0,
                                        pattern=[[-HEADS, P // HEADS], [-1, HEADS], [0, HD]],
                                        channel_multiplier=1).then_inc(consts, 1)
                nc.gpsimd.affine_select(out=head_of[:, :], in_=head_of[:, :], compare_op=ALU.is_ge, fill=0.0,
                                        base=0, pattern=[[-HD, HEADS]], channel_multiplier=1).then_inc(consts, 1)
                pool.wait_ge(consts, 3)
                nc.gpsimd.affine_select(out=head_of[:, :], in_=head_of[:, :], compare_op=ALU.is_ge, fill=0.0,
                                        base=HD - 1, pattern=[[HD, HEADS]], channel_multiplier=-1).then_inc(consts, 1)

            @block.tensor
            def _(pe):
                pe.wait_ge(consts, 1)
                landed = [0, 0]
                for n, (q, parts, _) in enumerate(small):
                    landed[q] += 16 * len(parts)
                    pe.wait_ge(raw_in[q], landed[q])
                    if n >= 2:
                        pe.wait_ge(raw_out, n - 1)
                    for m in range(sum(k for _, k in parts)):
                        last = nc.tensor.transpose(psum[:, 2 * q + m // 4, (m % 4) * P:(m % 4 + 1) * P],
                                                   raw[q][:, m * P:(m + 1) * P], ident[:, :])
                    last.then_inc(raw_tr, 1)

            @block.scalar
            def _(act):
                act.wait_ge(in_ready, 16 * (3 + B + TPS + 2 * NS))
                nc.scalar.mul(qkv_bias[:, 0:1], qkv_bias[:, 0:1], QSCALE)
                for n, (q, parts, dst) in enumerate(small):
                    act.wait_ge(raw_tr, n + 1)
                    for h in range(sum(k for _, k in parts) // 4):
                        last = nc.scalar.copy(dst[:, h * BANK:(h + 1) * BANK], psum[:, 2 * q + h, :])
                    last.then_inc(raw_out, 1)

        att_prod = carve(K, L)
        pv_prod = carve(K, L)
        xn = carve(TPS, C)
        xnT = carve(L)
        qT, kT, vT = carve(L), carve(L), carve(L)
        scores = carve(TPS, K, HEADS)
        probs = carve(TPS, K, HEADS)
        pT = [carve(L), carve(L)]
        att = carve(TPS, C)
        x2 = carve(TPS, C)
        stats = sb("stats", [P, TPS, 6])
        mv = sb("mv", [P, TPS, 2])
        std = sb("std", [P, TPS])
        rstd = sb("rstd", [P, TPS])
        top = sb("top", [P, TPS, HEADS])
        total = sb("total", [P, TPS, HEADS])

        def window_ops(j):
            def ends(a, shift):
                if shift is None:
                    return a.rearrange("p (s l) -> p s l", s=1)[:, :, 0:1], None
            mid = (lambda a: a[:, NS:L - NS], lambda a: a[:, j:j + L - 2 * NS])

            def tok_ends(a):
                w = a[:, 0:NS].unsqueeze(1)
                return bass.AP(tensor=w.tensor, offset=w.offset, ap=[w.ap[0], (L - NS, 2), (1, NS)])

            def key_ends(a):
                w = a[:, j:j + 1].unsqueeze(1)
                return bass.AP(tensor=w.tensor, offset=w.offset, ap=[w.ap[0], (L - K, 2), (0, NS)])
            return mid, (tok_ends, key_ends)

        pooled = [j for j in range(K) if j % 3 == 0]
        norm_var = sem("norm_var")
        norm_std = sem("norm_std")
        xn_done = sem("xn_done")
        xnT_ps = sem("xnT_ps")
        xnT_done = sem("xnT_done")
        qkv_ps = sem("qkv_ps")
        qkv_done = sem("qkv_done")
        qk_dve = sem("qk_dve")
        qk_pool = sem("qk_pool")
        score_ps = sem("score_ps")
        shifted = sem("shifted")
        exps = sem("exps")
        probs_done = sem("probs_done")
        pT_ps = sem("pT_ps")
        pT_done = sem("pT_done")
        spread_ps = sem("spread_ps")
        pv_done = sem("pv_done")
        proj_ps = sem("proj_ps")
        x2_done = sem("x2_done")
        x2_stored = sem("x2_stored")
        xn2_done = sem("xn2_done")
        xn2T_ps = sem("xn2T_ps")
        xn2T_done = sem("xn2T_done")
        score_v = psum[:, 4:6, :].rearrange("p a (t w) -> p (a t) w", t=2)[:, :, 0:WIN]

        def layer_norm(dve, src, dst, n):
            for t in range(TPS):
                nc.vector.bn_stats(stats[:, t, :], src(t))
            dve.drain()
            for t in range(TPS):
                last = nc.vector.bn_aggr(mv[:, t, :], stats[:, t, :])
            last.then_inc(norm_var, 1)
            dve.wait_ge(norm_std, n)
            nc.vector.reciprocal(rstd[:, :], std[:, :])
            dve.drain()
            for t in range(TPS):
                last = nc.vector.tensor_scalar(dst(t), src(t), mv[:, t, 0:1], rstd[:, t:t + 1],
                                               ALU.subtract, ALU.mult)
            return last

        with nc.Block() as block:
            @block.sync
            def _(sp):
                with sp.Fori(0, B) as b:
                    sp.wait_ge(x2_done, b + 1)
                    sp.dma_start(x2_dram[bass.ds(b, 1)].rearrange("b (t p) c -> p (b t) c", p=P), x2).then_inc(x2_stored, 16)

            @block.vector
            def _(dve):
                with dve.Fori(0, B) as b:
                    xb = x_all[:, bass.ds(b * TPS, TPS), :]
                    layer_norm(dve, lambda t: xb[:, t, :], lambda t: xn[:, t, :], 3 * b + 1).then_inc(xn_done, 1)
                    dve.wait_ge(qkv_done, 3 * b + 3)
                    for j in range(K):
                        if j not in pooled:
                            for q_of, k_of in window_ops(j):
                                last = nc.vector.tensor_tensor(q_of(att_prod[:, j, :]), q_of(qT), k_of(kT), ALU.mult)
                            last.then_inc(qk_dve, 1)
                    dve.wait_ge(score_ps, b + 1)
                    nc.vector.tensor_tensor(scores, score_v.rearrange("p t (k h) -> p t k h", h=HEADS),
                                            bias_win[:, :, :, :].rearrange("p t h k -> p t k h"), ALU.add)
                    dve.drain()
                    nc.vector.tensor_reduce(top[:, :, :], scores.rearrange("p t k h -> p t h k"), axis=AX_X, op=ALU.max)
                    dve.drain()
                    nc.vector.tensor_tensor(scores, scores, top[:, :, :].unsqueeze(2).to_broadcast([P, TPS, K, HEADS]),
                                            ALU.subtract).then_inc(shifted, 1)
                    dve.wait_ge(exps, b + 1)
                    nc.vector.tensor_reduce(total[:, :, :], probs.rearrange("p t k h -> p t h k"), axis=AX_X, op=ALU.add)
                    dve.drain()
                    nc.vector.reciprocal(total[:, :, :], total[:, :, :])
                    dve.drain()
                    nc.vector.tensor_tensor(probs, probs, total[:, :, :].unsqueeze(2).to_broadcast([P, TPS, K, HEADS]),
                                            ALU.mult).then_inc(probs_done, 1)
                    for j in range(K):
                        dve.wait_ge(spread_ps, K * b + j + 1)
                        for p_of, v_of in window_ops(j):
                            last = nc.vector.tensor_tensor(p_of(pv_prod[:, j, :]), p_of(psum[:, j % 4, :]), v_of(vT), ALU.mult)
                        last.then_inc(pv_done, 1)
                    dve.wait_ge(proj_ps, b + 1)
                    nc.vector.tensor_tensor(att, psum[:, 4, :].rearrange("p (t c) -> p t c", t=TPS),
                                            proj_bias[:, :].unsqueeze(1).to_broadcast([P, TPS, C]), ALU.add)
                    dve.drain()
                    layer_norm(dve, lambda t: att[:, t, :], lambda t: att[:, t, :], 3 * b + 2)
                    dve.drain()
                    nc.vector.tensor_tensor(x2, att, xb, ALU.add).then_inc(x2_done, 1)
                    dve.drain()
                    layer_norm(dve, lambda t: x2[:, t, :], lambda t: xn[:, t, :], 3 * b + 3).then_inc(xn2_done, 1)
                    dve.wait_ge(x2_stored, 16 * b + 16)
                    dve.wait_ge(xn2T_ps, b + 1)

            @block.gpsimd
            def _(pool):
                with pool.Fori(0, B) as b:
                    pool.wait_ge(qkv_done, 3 * b + 3)
                    for j in pooled:
                        for q_of, k_of in window_ops(j):
                            last = nc.gpsimd.tensor_tensor(q_of(att_prod[:, j, :]), q_of(qT), k_of(kT), ALU.mult)
                        last.then_inc(qk_pool, 1)

            @block.scalar
            def _(act):
                def roots(n):
                    act.wait_ge(norm_var, n)
                    nc.scalar.activation(std[:, :], mv[:, :, 1], ACT.Sqrt, bias=eps[:, 0:1]).then_inc(norm_std, 1)

                with act.Fori(0, B) as b:
                    roots(3 * b + 1)
                    act.wait_ge(xnT_ps, b + 1)
                    nc.scalar.copy(xnT, psum[:, 0, :]).then_inc(xnT_done, 1)
                    act.wait_ge(qkv_ps, b + 1)
                    for n, dst in enumerate((qT, kT, vT)):
                        nc.scalar.activation(dst, psum[:, 1 + n, :], ACT.Identity, scale=QSCALE if n == 0 else 1.0,
                                             bias=qkv_bias[:, n:n + 1]).then_inc(qkv_done, 1)
                    act.wait_ge(shifted, b + 1)
                    nc.scalar.activation(probs, scores, ACT.Exp).then_inc(exps, 1)
                    act.wait_ge(pT_ps, b + 1)
                    nc.scalar.copy(pT[0], psum[:, 6, :])
                    nc.scalar.copy(pT[1][0:WIN - P, :], psum[0:WIN - P, 7, :]).then_inc(pT_done, 1)
                    roots(3 * b + 2)
                    roots(3 * b + 3)
                    act.wait_ge(xn2T_ps, b + 1)
                    dst = xn2T[:, :].rearrange("p (t b) -> p t b", b=B)[:, :, bass.ds(b, 1)]
                    nc.scalar.copy(dst, psum[:, 5, :].unsqueeze(2)).then_inc(xn2T_done, 1)

            @block.tensor
            def _(pe):
                with pe.Fori(0, B) as b:
                    pe.wait_ge(xn_done, b + 1)
                    for t in range(TPS):
                        last = nc.tensor.transpose(psum[:, 0, t * P:(t + 1) * P], xn[:, t, :], ident[:, :])
                    last.then_inc(xnT_ps, 1)
                    pe.wait_ge(xnT_done, b + 1)
                    for n in range(3):
                        last = nc.tensor.matmul(psum[:, 1 + n, :], wqp[:, n * P:(n + 1) * P], xnT, start=True, stop=True)
                    last.then_inc(qkv_ps, 1)
                    nd, npool = 0, 0
                    for j in range(K):
                        if j in pooled:
                            npool += 1
                            pe.wait_ge(qk_pool, len(pooled) * b + npool)
                        else:
                            nd += 1
                            pe.wait_ge(qk_dve, (K - len(pooled)) * b + nd)
                        for t in range(TPS):
                            last = nc.tensor.matmul(score_v[:, t, j * HEADS:(j + 1) * HEADS],
                                                    att_prod[:, j, t * P:(t + 1) * P], head_of[:, :],
                                                    start=True, stop=True)
                    last.then_inc(score_ps, 1)
                    pe.wait_ge(probs_done, b + 1)
                    for t in range(TPS):
                        row = probs[:, t, :, :].rearrange("p k h -> p (k h)")
                        nc.tensor.transpose(psum[:, 6, t * P:(t + 1) * P], row[:, 0:P], ident[:, :])
                        last = nc.tensor.transpose(psum[0:WIN - P, 7, t * P:(t + 1) * P], row[:, P:WIN], ident[:, :])
                    last.then_inc(pT_ps, 1)
                    pe.wait_ge(pT_done, b + 1)

                    def project(j):
                        pe.wait_ge(pv_done, K * b + j + 1)
                        for t in range(TPS):
                            last = nc.tensor.matmul(psum[:, 4, t * P:(t + 1) * P], pv_prod[:, j, t * P:(t + 1) * P],
                                                    wqp[:, 3 * P:4 * P], start=(j == 0 and t == 0), stop=(j == K - 1),
                                                    skip_group_check=True)
                        return last

                    for j in range(K):
                        if j >= 4:
                            pe.wait_ge(pv_done, K * b + j - 3)
                        half, rows = (0, P) if j < P // HEADS else (1, WIN - P)
                        nc.tensor.matmul(psum[:, j % 4, :], spread[0:rows, j % (P // HEADS), :], pT[half][0:rows, :],
                                         start=True, stop=True).then_inc(spread_ps, 1)
                        if j >= 2:
                            project(j - 2)
                    project(K - 2)
                    project(K - 1).then_inc(proj_ps, 1)
                    pe.wait_ge(xn2_done, b + 1)
                    for t in range(TPS):
                        last = nc.tensor.transpose(psum[:, 5, t * P:(t + 1) * P], xn[:, t, :], ident[:, :])
                    last.then_inc(xn2T_ps, 1)
                    pe.wait_ge(xn2T_done, b + 1)

        max_in = [sem("max_in0"), sem("max_in1")]
        max_read = sem("max_read")
        top_row = sem("top_row")
        top_all = sem("top_all")
        hh_rows = w_hh.rearrange("(g m p) k -> m p g k", g=3, p=P)
        ih_rows = w_ih.rearrange("(gm p) k -> p gm k", p=P)
        with nc.Block() as block:
            @block.sync
            def _(sp):
                for g in range(3):
                    sp.dma_start(raw[0][:, g * G:(g + 1) * G].rearrange("p (m k) -> p m k", k=C),
                                 ih_rows[:, g * GM:(g + 1) * GM, :]).then_inc(max_in[0], 16)
                with sp.Fori(0, GM // 2) as i:
                    for q in range(2):
                        sp.wait_ge(max_read, 2 * i + 1)
                        sp.dma_start(raw[1 - q].rearrange("p (g k) -> p g k", g=3)[:, :, :],
                                     hh_rows[bass.ds(2 * i + q, 1)].rearrange("m p g k -> p (m g) k")
                                     ).then_inc(max_in[1 - q], 16)
                        if q == 0:
                            sp.wait_ge(max_read, 2 * i + 1)

            @block.vector
            def _(dve):
                dve.wait_ge(max_in[0], 48)
                nc.vector.tensor_reduce(w_max[:, GM:GM + 1], raw[0], axis=AX_X, op=ALU.max,
                                        apply_absolute_value=True).then_inc(max_read, 1)
                with dve.Fori(0, GM // 2) as i:
                    for q in range(2):
                        dve.wait_ge(max_in[1 - q], 16 * i + (16 if q == 0 else 64))
                        nc.vector.tensor_reduce(w_max[:, bass.ds(2 * i + q, 1)], raw[1 - q], axis=AX_X, op=ALU.max,
                                                apply_absolute_value=True).then_inc(max_read, 1)
                dve.drain()
                nc.vector.tensor_reduce(w_top[:, :], w_max[:, :], axis=AX_X, op=ALU.max).then_inc(top_row, 1)
                dve.wait_ge(top_all, 1)
                nc.vector.tensor_scalar(w_all[:, :], w_all[:, :], 2.0 ** -100, None, ALU.max)
                dve.drain()
                nc.vector.tensor_scalar(w_exp[:, :], w_all[:, :].bitcast(U32), 0x7F800000, None, ALU.bitwise_and)
                dve.drain()
                nc.vector.tensor_scalar(w_scale[:, :], w_exp[:, :], -1.0, float(268 << 23), ALU.mult, ALU.add)
                nc.vector.tensor_scalar(w_unscale[:, :], w_exp[:, :], float(14 << 23), None, ALU.subtract)

            @block.gpsimd
            def _(pool):
                pool.wait_ge(top_row, 1)
                nc.gpsimd.partition_all_reduce(w_all[:, :], w_top[:, :], P, RMAX).then_inc(top_all, 1)

        rec_in = [sem("rec_in0"), sem("rec_in1")]
        rec_tr = sem("rec_tr")
        rec_hi = sem("rec_hi")
        rec_lo = sem("rec_lo")
        PLACE = (1, 2, 0)
        with nc.Block() as block:
            @block.sync
            def _(sp):
                for g in range(3):
                    sp.dma_start(raw[1][:, g * G:(g + 1) * G].rearrange("p (m k) -> p m k", k=C),
                                 ih_rows[:, g * GM:(g + 1) * GM, :]).then_inc(rec_in[1], 16)
                with sp.Fori(0, GM // 2) as i:
                    for q in range(2):
                        sp.wait_ge(rec_tr, 6 * i + (1 if q == 0 else 3))
                        sp.dma_start(raw[q].rearrange("p (g k) -> p g k", g=3)[:, :, :],
                                     hh_rows[bass.ds(i + HALF * q, 1)].rearrange("m p g k -> p (m g) k")
                                     ).then_inc(rec_in[q], 16)

            def by_group(g, m):
                return psum[:, 2 * g + m // 4, :].rearrange("p (j c u) -> p c j u", j=4, u=32)[:, m % 4]

            def banks(g):
                return psum[:, 2 * g:2 * g + 2, :].rearrange("p a (c r) -> p (a c) r", r=P)

            def in_groups(g):
                return psum[:, 2 * g:2 * g + 2, :].rearrange("p a (k u) -> p (a k) u", u=32)

            def halves(g, h):
                return psum[:, 2 * g + h, :].rearrange("p (j r) -> p j r", j=4)

            @block.tensor
            def _(pe):
                pe.wait_ge(rec_in[1], 48)
                for g in range(3):
                    for m in range(GM):
                        last = nc.tensor.transpose(by_group(g, m), raw[1][:, (g * GM + m) * P:(g * GM + m + 1) * P], ident[:, :])
                    last.then_inc(rec_tr, 1)
                with pe.Fori(0, GM // 2) as i:
                    for q in range(2):
                        pe.wait_ge(rec_in[q], 16 * i + (16 if q == 0 else 64))
                        for g in range(3):
                            pe.wait_ge(rec_lo, 6 * i + 3 * q + g + 1)
                            for c in range(CH):
                                last = nc.tensor.transpose(banks(g)[:, c, :], raw[q][:, g * G + c * P:g * G + (c + 1) * P], ident[:, :])
                            last.then_inc(rec_tr, 1)

            @block.scalar
            def _(act):
                for g in range(3):
                    act.wait_ge(rec_tr, g + 1)
                    for h in range(2):
                        last = nc.scalar.activation(w_ih_s[:, 0, h, :, PLACE[g], :], halves(g, h), ACT.Copy, scale=scale_f[:, 0:1])
                    last.then_inc(rec_hi, 1)
                with act.Fori(0, GM // 2) as i:
                    for q in range(2):
                        for g in range(3):
                            act.wait_ge(rec_tr, 6 * i + 3 * q + g + 4)
                            nc.scalar.activation(w_hh_s[:, 0, q, :, g, bass.ds(i * 32, 32)],
                                                 in_groups(g), ACT.Copy, scale=scale_f[:, 0:1]).then_inc(rec_hi, 1)

            @block.vector
            def _(dve):
                for g in range(3):
                    dve.wait_ge(rec_hi, g + 1)
                    for h in range(2):
                        last = nc.vector.scalar_tensor_tensor(w_ih_s[:, 1, h, :, PLACE[g], :], halves(g, h), scale_f[:, 0:1],
                                                              w_ih_s[:, 0, h, :, PLACE[g], :], ALU.mult, ALU.subtract)
                    last.then_inc(rec_lo, 1)
                with dve.Fori(0, GM // 2) as i:
                    for q in range(2):
                        for g in range(3):
                            dve.wait_ge(rec_hi, 6 * i + 3 * q + g + 4)
                            hi, lo = (w_hh_s[:, s, q, :, g, bass.ds(i * 32, 32)] for s in range(2))
                            nc.vector.scalar_tensor_tensor(lo, in_groups(g), scale_f[:, 0:1], hi,
                                                           ALU.mult, ALU.subtract).then_inc(rec_lo, 1)

        HB = HALF * B
        NSHIFT = NEXP // 2 + 1
        WRAP = NEXP + NSHIFT - 1
        h_parts = sb("h_parts", [P, 2, CH, 4 * B], BF16)
        x_now = sb("x_now", [P, 2, 4 * B], BF16)
        h_full = sb("h_full", [P, 2, CH * B])
        turned = sb("turned", [P, 2, 4, P])
        gates = sb("gates", [P, 2, 4, HB])
        rz = sb("rz", [P, 2, 2, HB])
        pre_n = sb("pre_n", [P, 2, 2, HB])
        n_act = sb("n_act", [P, 2, HB])
        keep = sb("keep", [P, 2, HB])
        not_z = sb("not_z", [P, 2, HB])
        fresh = sb("fresh", [P, 2, HB])
        rest = sb("rest", [P, 2, HB])
        x_mean = sb("x_mean", [P, B])
        history = sb("history", [P, CH, SP_T, B])
        x_tile = sb("x_tile", [P, P])
        routes = sb("routes", [P, 2, WRAP, P])
        products = sb("products", [P, NSHIFT, P])
        gram = sb("gram", [P, NT + 1, NEXP, NSHIFT + 2])
        x_rest = routes[:, :, :, :].rearrange("p a e d -> p (a e d)")[:, 0:TOK // 4]
        mean_done = sem("mean_done")
        h0_ps = sem("h0_ps")
        cleared = sem("cleared")
        x_staged = sem("x_staged")
        x_used = sem("x_used")

        def two(name):
            return [sem(name + "A"), sem(name + "B")]

        h_ready, bank_free, gates_ps = two("h_ready"), two("bank_free"), two("gates_ps")
        rz_turned, gates_in, n_in, rz_done = two("rz_turned"), two("gates_in"), two("n_in"), two("rz_done")
        hn_scaled, pre_done, n_done, keep_done = two("hn_scaled"), two("pre_done"), two("n_done"), two("keep_done")
        fresh_done, first_part, second_part = two("fresh_done"), two("first_part"), two("second_part")
        kept = sem("kept")
        tile_ps = sem("tile_ps")
        tile_read = sem("tile_read")
        tile_staged = sem("tile_staged")
        multiplied = sem("multiplied")
        dots_half = sem("dots_half")
        dots_done = sem("dots_done")

        def part(parts, i):
            return parts[:, :, i * B:(i + 1) * B]

        def by_chunk(a):
            return a.rearrange("p (c b) -> p c b", b=B)

        def tile_products(pe):
            for c in range(CH):
                nc.tensor.transpose(psum[:, 4 + c // 4, (c % 4) * P:(c % 4 + 1) * P],
                                    history[:, c, :, :].rearrange("p t b -> p (t b)"), ident[:, :])
            for h in range(2):
                last = nc.tensor.matmul(psum[:, 6 + h, :], x_tile[:, :], exprT[:, h * BANK:(h + 1) * BANK], start=True, stop=True)
            return last

        def tile_copies(act):
            for h in range(2):
                nc.scalar.copy(routes[:, 0, 4 * h:4 * h + 4, :].rearrange("p e d -> p (e d)"), psum[:, 4 + h, :])
            nc.scalar.copy(routes[:, 0, NEXP:WRAP, :].rearrange("p e d -> p (e d)"), psum[:, 4, :])
            for h in range(2):
                last = nc.scalar.copy(routes[:, 1, 4 * h:4 * h + 4, :].rearrange("p e d -> p (e d)"), psum[:, 6 + h, :])
            return last

        def expr_dots(slot, e):
            here = routes[:, :, bass.ds(e, 1), :].rearrange("p a e d -> p a (e d)")
            return nc.vector.tensor_tensor(products[:, 0:2, :], here, routes[:, 1, bass.ds(e, 1), :].to_broadcast([P, 2, P]), ALU.mult)

        def state_dots(slot, e):
            return nc.vector.tensor_tensor(products[:, :, :], routes[:, 0, bass.ds(e, 1), :].to_broadcast([P, NSHIFT, P]),
                                           routes[:, 0, bass.ds(e, NSHIFT), :], ALU.mult)

        def sum_dots(slot, e, lo, n):
            dst = gram[:, bass.ds(slot, 1), bass.ds(e, 1), lo:lo + n].rearrange("p a e s -> p (a e s)")
            return nc.vector.tensor_reduce(dst, products[:, 0:n, :], axis=AX_X, op=ALU.add)

        with nc.Block() as block:
            @block.gpsimd
            def _(pool):
                nc.gpsimd.memset(h_parts[:, :, :, :], 0.0).then_inc(cleared, 1)
                nc.gpsimd.memset(x_now[:, :, :], 0.0)
                nc.gpsimd.memset(x_parts[:, L, :], 0.0)
                nc.gpsimd.memset(history[:, :, :, :], 0.0)
                nc.gpsimd.memset(x_tile[:, :], 0.0)

            @block.vector
            def _(dve):
                nc.vector.tensor_reduce(x_mean[:, :], xn2T[:, :].rearrange("p (t b) -> p b t", b=B), axis=AX_X, op=ALU.add)
                dve.drain()
                nc.vector.tensor_scalar(x_mean[:, :], x_mean[:, :], 1.0 / L, None, ALU.mult).then_inc(mean_done, 1)
                for i in range(4):
                    n = L // 4
                    src = xn2T[:, i * n * B:(i + 1) * n * B].rearrange("p (t b) -> p t b", b=B)
                    left = x_rest.rearrange("p (t b) -> p t b", b=B)
                    xp = [x_parts[:, i * n:(i + 1) * n, s * B:(s + 1) * B] for s in range(3)]
                    nc.vector.tensor_copy(xp[0], src)
                    dve.drain()
                    nc.vector.tensor_tensor(left, src, xp[0], ALU.subtract)
                    nc.vector.tensor_tensor(xp[1], src, xp[0], ALU.subtract)
                    dve.drain()
                    nc.vector.tensor_tensor(xp[2], left, xp[1], ALU.subtract)
                    dve.drain()
                dve.wait_ge(h0_ps, 1)
                dve.wait_ge(cleared, 1)
                nc.vector.tensor_tensor(by_chunk(h_full[:, 0, :]), by_chunk(psum[:, 0, 0:CH * B]),
                                        ctx_bias[:, :].unsqueeze(2).to_broadcast([P, CH, B]), ALU.add)
                dve.drain()
                full = by_chunk(h_full[:, 0, :])
                left = rest[:, :, :].rearrange("p h (c b) -> p (h c) b", b=B)
                parts = h_parts[:, 0, :, :]
                nc.vector.tensor_copy(part(parts, 0), full)
                dve.drain()
                nc.vector.tensor_tensor(left, full, part(parts, 0), ALU.subtract)
                nc.vector.tensor_tensor(part(parts, 1), full, part(parts, 0), ALU.subtract)
                dve.drain()
                nc.vector.tensor_tensor(part(parts, 2), left, part(parts, 1), ALU.subtract)
                dve.drain()
                for half in range(2):
                    dve.sem_inc(h_ready[half], 1)
                    dve.sem_inc(bank_free[half], 2)
                dve.sem_inc(x_used, 2)
                dve.sem_inc(kept, 2)
                dve.sem_inc(tile_staged, 1)
                dve.sem_inc(tile_read, 1)
                dve.sem_inc(dots_done, 1)

            @block.tensor
            def _(pe):
                pe.wait_ge(mean_done, 1)
                for c in range(CH):
                    last = nc.tensor.matmul(psum[:, 0, c * B:(c + 1) * B], ctxT[:, c * P:(c + 1) * P], x_mean[:, :], start=True, stop=True)
                last.then_inc(h0_ps, 1)

        with nc.Block() as block:
            PAIRS = SP_T // 2
            EARLY = 3

            def over_steps(eng, body):
                with eng.Fori(0, NT) as n:
                    body(n, 0, True)
                    with eng.Fori(1, PAIRS) as i:
                        body(n, i, False)

            @block.gpsimd
            def _(pool):
                nc.gpsimd.tensor_copy(x_now[:, 0, 0:3 * B], x_parts[:, 0, :]).then_inc(x_staged, 1)

                def pair(n, i, first):
                    t0 = n * SP_T + 2 * i
                    for q in range(2):
                        pool.wait_ge(x_used, t0 + q + 2)
                        nc.gpsimd.tensor_copy(x_now[:, 1 - q, 0:3 * B].unsqueeze(1), x_parts[:, bass.ds(t0 + q + 1, 1), :]).then_inc(x_staged, 1)
                        for half in range(2):
                            pool.wait_ge(rz_done[half], t0 + q + 1)
                            nc.gpsimd.tensor_tensor(keep[:, half, :], rz[:, half, 1, :], h_full[:, q, half * HB:(half + 1) * HB], ALU.mult)
                            nc.gpsimd.tensor_scalar(not_z[:, half, :], rz[:, half, 1, :], -1.0, 1.0, ALU.mult, ALU.add).then_inc(keep_done[half], 1)
                    if first:
                        nc.gpsimd.tensor_copy(x_tile[:, :], xn2T[:, bass.ds(n * P, P)]).then_inc(tile_staged, 1)

                over_steps(pool, pair)

            @block.tensor
            def _(pe):
                def state_share(q, half, chunks):
                    for c in chunks:
                        for s in range(2):
                            for j in range(4):
                                last = nc.tensor.matmul(psum[32 * j:32 * j + 32, 2 * q + half, P:4 * P], h_parts[:, q, c, :],
                                                        w_hh_s[:, s, half, 4 * c + j, :, :].rearrange("p g r -> p (g r)"),
                                                        start=False, stop=(c == CH - 1 and s == 1), skip_group_check=True)
                    return last

                def pair(n, i, first):
                    t0 = n * SP_T + 2 * i
                    for q in range(2):
                        pe.wait_ge(x_staged, t0 + q + 1)
                        for half in range(2):
                            pe.wait_ge(bank_free[half], t0 + q + 1)
                            for s in range(2):
                                for j in range(4):
                                    last = nc.tensor.matmul(psum[32 * j:32 * j + 32, 2 * q + half, 0:3 * P], x_now[:, q, :],
                                                            w_ih_s[:, s, half, j, :, :].rearrange("p g r -> p (g r)"),
                                                            start=(s == 0), stop=False, skip_group_check=True)
                        last.then_inc(x_used, 1)
                        pe.wait_ge(h_ready[0], t0 + q + 1)
                        state_share(q, 0, range(0, HALF))
                        state_share(q, 1, range(0, EARLY))
                        pe.wait_ge(h_ready[1], t0 + q + 1)
                        state_share(q, 0, range(HALF, CH)).then_inc(gates_ps[0], 1)
                        state_share(q, 1, range(EARLY, CH)).then_inc(gates_ps[1], 1)
                        if first and q == 0:
                            pe.wait_ge(kept, n * SP_T + 2)
                            pe.wait_ge(tile_staged, n + 1)
                            pe.wait_ge(tile_read, n + 1)
                            tile_products(pe).then_inc(tile_ps, 1)

                over_steps(pe, pair)

            @block.vector
            def _(dve):
                def summed(half, g):
                    return nc.vector.tensor_reduce(by_chunk(gates[:, half, g:g + 2, :].rearrange("p g k -> p (g k)")),
                                                   turned[:, half, g:g + 2, :].rearrange("p g (k s b) -> p (g k) b s", s=4, b=B)[:, :, :, 0:3],
                                                   axis=AX_X, op=ALU.add)

                def turn(t1, q, half):
                    bank = psum[:, 2 * q + half, :].rearrange("p (g r) -> p g r", g=4)
                    dve.wait_ge(gates_ps[half], t1)
                    if half == 0:
                        dve.wait_ge(kept, t1)
                    nc.vector.transpose(turned[:, half, 0:2, :], bank[:, 1:3, :]).then_inc(rz_turned[half], 1)
                    nc.vector.transpose(turned[:, half, 2:4, :], bank[:, 0:4:3, :]).then_inc(bank_free[half], 1)

                def before_tanh(t1, q, half):
                    dve.wait_ge(rz_turned[half], t1)
                    summed(half, 0).then_inc(gates_in[half], 1)
                    dve.wait_ge(bank_free[half], t1 + 2)
                    summed(half, 2).then_inc(n_in[half], 1)
                    dve.wait_ge(rz_done[half], t1)
                    dve.wait_ge(n_in[half], t1)
                    nc.vector.tensor_tensor(pre_n[:, half, 0, :], rz[:, half, 0, :], gates[:, half, 3, :], ALU.mult).then_inc(hn_scaled[half], 1)
                    dve.wait_ge(hn_scaled[half], t1)
                    nc.vector.tensor_tensor(pre_n[:, half, 1, :], pre_n[:, half, 0, :], gates[:, half, 2, :], ALU.add).then_inc(pre_done[half], 1)

                def after_tanh(t1, q, half):
                    dve.wait_ge(n_done[half], t1)
                    dve.wait_ge(keep_done[half], t1)
                    full = h_full[:, 1 - q, half * HB:(half + 1) * HB]
                    parts = h_parts[:, 1 - q, half * HALF:(half + 1) * HALF, :]
                    nc.vector.tensor_tensor(fresh[:, half, :], not_z[:, half, :], n_act[:, half, :], ALU.mult).then_inc(fresh_done[half], 1)
                    dve.wait_ge(fresh_done[half], t1)
                    nc.vector.tensor_tensor(full, fresh[:, half, :], keep[:, half, :], ALU.add)
                    nc.vector.tensor_tensor(part(parts, 0), by_chunk(fresh[:, half, :]), by_chunk(keep[:, half, :]), ALU.add).then_inc(first_part[half], 1)
                    dve.wait_ge(first_part[half], t1)
                    nc.vector.tensor_tensor(by_chunk(rest[:, half, :]), by_chunk(full), part(parts, 0), ALU.subtract)
                    nc.vector.tensor_tensor(part(parts, 1), by_chunk(full), part(parts, 0), ALU.subtract).then_inc(second_part[half], 1)
                    dve.wait_ge(second_part[half], t1)
                    nc.vector.tensor_tensor(part(parts, 2), by_chunk(rest[:, half, :]), part(parts, 1), ALU.subtract).then_inc(h_ready[half], 1)

                def pair(n, i, first):
                    t0 = n * SP_T + 2 * i
                    for q in range(2):
                        t1 = t0 + q + 1
                        turn(t1, q, 0)
                        before_tanh(t1, q, 0)
                        after_tanh(t1, q, 0)
                        turn(t1, q, 1)
                        before_tanh(t1, q, 1)
                        after_tanh(t1, q, 1)
                        if q == 0:
                            dve.wait_ge(tile_read, n + 2)
                            expr_dots(n, i).then_inc(multiplied, 1)
                            dve.wait_ge(multiplied, t0 + 1)
                            sum_dots(n, i, NSHIFT, 2).then_inc(dots_half, 1)
                        else:
                            dve.wait_ge(dots_half, n * PAIRS + i + 1)
                            state_dots(n, i).then_inc(multiplied, 1)
                            dve.wait_ge(multiplied, t0 + 2)
                            sum_dots(n, i, 0, NSHIFT).then_inc(dots_done, 1)

                over_steps(dve, pair)

            @block.scalar
            def _(act):
                def pair(n, i, first):
                    t0 = n * SP_T + 2 * i
                    for q in range(2):
                        t1 = t0 + q + 1
                        for half in range(2):
                            act.wait_ge(gates_in[half], t1)
                            nc.scalar.activation(rz[:, half, :, :], gates[:, half, 0:2, :], ACT.Sigmoid,
                                                 scale=unscale_f[:, 0:1]).then_inc(rz_done[half], 1)
                            act.wait_ge(pre_done[half], t1)
                            nc.scalar.activation(n_act[:, half, :], pre_n[:, half, 1, :], ACT.Tanh,
                                                 scale=unscale_f[:, 0:1]).then_inc(n_done[half], 1)
                        act.wait_ge(h_ready[1], t1 + 1)
                        act.wait_ge(tile_ps, n + 1)
                        nc.scalar.copy(history[:, :, bass.ds(2 * i + q, 1), :].rearrange("p c t b -> p c (t b)"),
                                       by_chunk(h_full[:, 1 - q, :])).then_inc(kept, 1)
                        if first and q == 0:
                            act.wait_ge(dots_done, n * PAIRS + 1)
                            tile_copies(act).then_inc(tile_read, 1)

                over_steps(act, pair)

        taken[0] = 0
        expT = carve(NE, 6, P)
        mix = carve(NT, NEXP)
        ew_in = [sem("ew_in0"), sem("ew_in1")]
        ew_tr = sem("ew_tr")
        ew_out = sem("ew_out")
        loads = []
        for kind, (w, sw) in enumerate(((gate_w, sgate_w), (up_w, sup_w), (down_w, sdown_w))):
            for lo in range(0, NEXP, 4):
                loads.append((kind, lo, 4, w[lo:lo + 4]))
            loads.append((kind, NEXP, 1, sw.unsqueeze(0)))

        def rows_of(kind, w):
            if kind < 2:
                return w.rearrange("e (f p) k -> p (e f) k", p=P)
            return w.rearrange("e p (f k) -> p (e f) k", k=P)

        with nc.Block() as block:
            @block.sync
            def _(sp):
                for n, (kind, lo, ne, w) in enumerate(loads):
                    if n >= 2:
                        sp.wait_ge(ew_tr, n - 1)
                    if kind < 2:
                        sp.dma_start(raw[n % 2][:, 0:2 * ne * P].rearrange("p (e k) -> p e k", k=P), rows_of(kind, w)).then_inc(ew_in[n % 2], 16)
                    else:
                        sp.dma_start(raw[n % 2][:, 0:2 * ne * P].rearrange("p (e k) -> p e k", k=FF), w.rearrange("e p k -> p e k")).then_inc(ew_in[n % 2], 16)

            @block.tensor
            def _(pe):
                for n, (kind, lo, ne, w) in enumerate(loads):
                    pe.wait_ge(ew_in[n % 2], 16 * (n // 2 + 1))
                    if n >= 2:
                        pe.wait_ge(ew_out, n - 1)
                    for m in range(2 * ne):
                        last = nc.tensor.transpose(psum[:, 2 * (n % 2) + m // 4, (m % 4) * P:(m % 4 + 1) * P],
                                                   raw[n % 2][:, m * P:(m + 1) * P], ident[:, :])
                    last.then_inc(ew_tr, 1)

            @block.scalar
            def _(act):
                for n, (kind, lo, ne, w) in enumerate(loads):
                    act.wait_ge(ew_tr, n + 1)
                    for h in range((ne + 1) // 2):
                        k = min(2, ne - 2 * h)
                        last = nc.scalar.copy(expT[:, lo + 2 * h:lo + 2 * h + k, 2 * kind:2 * kind + 2, :],
                                              psum[:, 2 * (n % 2) + h, 0:2 * k * P].rearrange("p (e f r) -> p e f r", e=k, f=2))
                    last.then_inc(ew_out, 1)

        last_ps = sem("last_ps")
        last_read = sem("last_read")
        with nc.Block() as block:
            @block.tensor
            def _(pe):
                tile_products(pe).then_inc(last_ps, 1)

            @block.scalar
            def _(act):
                act.wait_ge(last_ps, 1)
                tile_copies(act).then_inc(last_read, 1)

            @block.vector
            def _(dve):
                dve.wait_ge(last_read, 1)
                for e in range(NEXP):
                    expr_dots(NT, e)
                    dve.drain()
                    sum_dots(NT, e, NSHIFT, 2)
                    dve.drain()
                    state_dots(NT, e)
                    dve.drain()
                    sum_dots(NT, e, 0, NSHIFT)
                    dve.drain()

        dots = gram[:, 1:NT + 1, :, :]
        wrap = NEXP // 2

        def wide(name, n=NEXP):
            return carve(NT, n)
        length = wide("length")
        inv12 = wide("inv12", NEXP + wrap)
        e_len = wide("e_len")
        gsq = carve(NT, NEXP + wrap)
        row_sq = wide("row_sq")
        tmp = wide("tmp")
        tmp2 = wide("tmp2")
        score = wide("score")
        best = wide("best")
        best_at = carve(NT, NEXP).bitcast(U32)
        best_f = wide("best_f")
        places = carve(NEXP)
        pen = carve(4)
        pair = carve(NT, 4)
        r1 = sem("lengths_sq")
        r2 = sem("lengths_rt")
        r3 = sem("row_sum")
        r4 = sem("row_root")
        r5 = sem("pen_part")
        r6 = sem("pen_sum")
        r7 = sem("places_set")
        r8 = sem("gap_done")
        r9 = sem("gap_exp")
        with nc.Block() as block:
            @block.scalar
            def _(act):
                nc.scalar.activation(length, dots[:, :, :, 0], ACT.Sqrt)
                nc.scalar.activation(e_len, dots[:, :, :, NSHIFT + 1], ACT.Sqrt).then_inc(r2, 1)
                act.wait_ge(r3, 1)
                nc.scalar.activation(tmp, row_sq, ACT.Sqrt).then_inc(r4, 1)
                act.wait_ge(r8, 1)
                nc.scalar.activation(pair[:, :, 1:2], pair[:, :, 0:1], ACT.Exp).then_inc(r9, 1)

            @block.gpsimd
            def _(pool):
                nc.gpsimd.iota(places, pattern=[[1, NEXP]], base=0, channel_multiplier=0, allow_small_or_imprecise_dtypes=True).then_inc(r7, 1)
                pool.wait_ge(r5, 1)
                nc.gpsimd.partition_all_reduce(pen[:, 1:2], pen[:, 0:1], P, RADD).then_inc(r6, 1)

            @block.vector
            def _(dve):
                v = nc.vector

                def tt(o, a, b_, op):
                    r = v.tensor_tensor(o, a, b_, op)
                    dve.drain()
                    return r

                def ts(o, a, s1, s2, op0, op1=None):
                    r = v.tensor_scalar(o, a, s1, s2, op0, op1) if op1 is not None else v.tensor_scalar(o, a, s1, s2, op0)
                    dve.drain()
                    return r

                dve.wait_ge(r2, 1)
                inv = inv12[:, :, 0:NEXP]
                ts(inv, length, 1e-12, None, ALU.max)
                v.reciprocal(inv, inv)
                dve.drain()
                v.tensor_copy(inv12[:, :, NEXP:], inv12[:, :, 0:wrap])
                dve.drain()
                tt(tmp, dots[:, :, :, 0], inv, ALU.mult)
                tt(tmp, tmp, inv, ALU.mult)
                ts(tmp, tmp, 1.0, None, ALU.subtract)
                tt(row_sq, tmp, tmp, ALU.mult)
                for s in range(1, wrap + 1):
                    n = NEXP if s < wrap else wrap
                    g = gsq[:, :, wrap:wrap + n]
                    tt(g, dots[:, :, 0:n, s], inv12[:, :, 0:n], ALU.mult)
                    tt(g, g, inv12[:, :, s:s + n], ALU.mult)
                    tt(g, g, g, ALU.mult)
                    tt(row_sq[:, :, 0:n], row_sq[:, :, 0:n], g, ALU.add)
                    first = min(n, NEXP - s)
                    tt(row_sq[:, :, s:s + first], row_sq[:, :, s:s + first], g[:, :, 0:first], ALU.add)
                    if first < n:
                        tt(row_sq[:, :, 0:n - first], row_sq[:, :, 0:n - first], g[:, :, first:n], ALU.add)
                dve.drain().then_inc(r3, 1)
                dve.wait_ge(r4, 1)
                ts(tmp, tmp, 1e-12, None, ALU.max)
                v.reciprocal(tmp, tmp)
                dve.drain()
                tt(tmp2, row_sq, tmp, ALU.mult)
                tt(tmp2, tmp2, tmp, ALU.mult)
                v.tensor_reduce(pen[:, 0:1], tmp2.rearrange("p t e -> p (t e)"), axis=AX_X, op=ALU.add).then_inc(r5, 1)
                dve.drain()
                tt(tmp2, length, inv, ALU.mult)
                ts(tmp2, tmp2, 1e-8, None, ALU.max)
                ts(tmp, e_len, 1e-8, None, ALU.max)
                tt(tmp, tmp, tmp2, ALU.mult)
                v.reciprocal(tmp, tmp)
                dve.drain()
                tt(score, dots[:, :, :, NSHIFT], inv, ALU.mult)
                tt(score, score, tmp, ALU.mult)
                ts(score, score, -1.0, 1.0, ALU.mult, ALU.add)
                dve.wait_ge(r6, 1)
                ts(pen[:, 2:3], pen[:, 1:2], 1.0 / TOK, 1.0, ALU.mult, ALU.add)
                ts(score, score, pen[:, 2:3], None, ALU.mult)
                for n in range(NT):
                    v.max(best[:, n, :], score[:, n, :])
                dve.drain()
                for n in range(NT):
                    v.max_index(best_at[:, n, :], best[:, n, :], score[:, n, :])
                dve.drain()
                v.tensor_copy(best_f, best_at)
                tt(pair[:, :, 0:1], best[:, :, 1:2], best[:, :, 0:1], ALU.subtract)
                dve.drain().then_inc(r8, 1)
                dve.wait_ge(r9, 1)
                dve.wait_ge(r7, 1)
                ts(pair[:, :, 2:3], pair[:, :, 1:2], 1.0, None, ALU.add)
                v.reciprocal(pair[:, :, 2:3], pair[:, :, 2:3])
                dve.drain()
                tt(pair[:, :, 3:4], pair[:, :, 1:2], pair[:, :, 2:3], ALU.mult)
                every = places.unsqueeze(1).to_broadcast([P, NT, NEXP])
                tt(tmp, every, best_f[:, :, 0:1].to_broadcast([P, NT, NEXP]), ALU.is_equal)
                tt(mix, tmp, pair[:, :, 2:3].to_broadcast([P, NT, NEXP]), ALU.mult)
                tt(tmp, every, best_f[:, :, 1:2].to_broadcast([P, NT, NEXP]), ALU.is_equal)
                tt(tmp, tmp, pair[:, :, 3:4].to_broadcast([P, NT, NEXP]), ALU.mult)
                tt(mix, mix, tmp, ALU.add)

        QT = BANK // P
        RING = 3
        UNITS = NE * FC
        hid_a = [carve(BANK) for _ in range(RING)]
        hid = [carve(BANK) for _ in range(2 * FC)]
        acc = carve(QT, C)
        x2_in = carve(QT, C)
        y_out = carve(QT, C)
        x2t_in = sem("x2t_in")
        gate_ps = sem("gate_ps")
        silu_done = sem("silu_done")
        hid_done = sem("hid_done")
        down_ps = sem("down_ps")
        down_read = sem("down_read")
        f_var = sem("f_var")
        f_std = sem("f_std")
        y_done = sem("y_done")
        y_stored = sem("y_stored")

        def token_rows(dram, tile):
            return dram.rearrange("b t c -> t b c")[bass.ds(tile * SP_T, SP_T)]

        with nc.Block() as block:
            @block.sync
            def _(sp):
                sp.sem_inc(y_done, 1)
                with sp.Fori(0, NT // QT) as i:
                    sp.wait_ge(y_done, i + 1)
                    for t in range(QT):
                        sp.dma_start(x2_in[:, t, :], token_rows(x2_dram, i * QT + t)).then_inc(x2t_in, 16)
                    sp.wait_ge(y_done, i + 2)
                    for t in range(QT):
                        sp.dma_start(token_rows(out, i * QT + t), y_out[:, t, :]).then_inc(y_stored, 16)
                sp.wait_ge(y_stored, 16 * NT)

            @block.tensor
            def _(pe):
                pe.sem_inc(hid_done, RING)
                pe.sem_inc(down_read, 2)
                with pe.Fori(0, NT // QT) as i:
                    toks = xn2T[:, bass.ds(i * BANK, BANK)]

                    def down(e):
                        pe.wait_ge(hid_done, UNITS * i + FC * (e + 1) + RING)
                        pe.wait_ge(down_read, NE * i + e + (2 if e == 0 else 1))
                        for t in range(QT):
                            for f in range(FC):
                                last = nc.tensor.matmul(psum[:, 6 + e % 2, t * P:(t + 1) * P],
                                                        hid[(FC * e + f) % (2 * FC)][:, t * P:(t + 1) * P],
                                                        expT[:, e, 4 + f, :], start=(f == 0), stop=(f == FC - 1))
                        last.then_inc(down_ps, 1)

                    for e in range(NE):
                        for f in range(FC):
                            u = FC * e + f
                            pe.wait_ge(hid_done, UNITS * i + u + 1)
                            for k in range(2):
                                last = nc.tensor.matmul(psum[:, 2 * (u % RING) + k, :], expT[:, e, FC * k + f, :], toks,
                                                        start=True, stop=True)
                            last.then_inc(gate_ps, 1)
                        if e >= 1:
                            down(e - 1)
                    down(NE - 1)

            @block.scalar
            def _(act):
                with act.Fori(0, NT // QT) as i:
                    for u in range(UNITS):
                        act.wait_ge(gate_ps, UNITS * i + u + 1)
                        act.wait_ge(hid_done, UNITS * i + u + 1)
                        nc.scalar.activation(hid_a[u % RING], psum[:, 2 * (u % RING), :], ACT.Silu).then_inc(silu_done, 1)
                    act.wait_ge(f_var, i + 1)
                    nc.scalar.activation(std[:, :], mv[:, :, 1], ACT.Sqrt, bias=eps[:, 0:1]).then_inc(f_std, 1)

            @block.vector
            def _(dve):
                with dve.Fori(0, NT // QT) as i:
                    def collect(e):
                        dve.wait_ge(down_ps, NE * i + e + 1)
                        for t in range(QT):
                            y = psum[:, 6 + e % 2, t * P:(t + 1) * P]
                            if e == 0:
                                w = mix[:, bass.ds(i * QT + t, 1), e:e + 1].rearrange("p a b -> p (a b)")
                                last = nc.vector.tensor_scalar(acc[:, t, :], y, w, None, ALU.mult)
                            elif e < NEXP:
                                w = mix[:, bass.ds(i * QT + t, 1), e:e + 1].rearrange("p a b -> p (a b)")
                                last = nc.vector.scalar_tensor_tensor(acc[:, t, :], y, w, acc[:, t, :], ALU.mult, ALU.add)
                            else:
                                last = nc.vector.tensor_tensor(acc[:, t, :], y, acc[:, t, :], ALU.add)
                        last.then_inc(down_read, 1)
                        dve.drain()

                    for e in range(NE):
                        for f in range(FC):
                            u = FC * e + f
                            dve.wait_ge(silu_done, UNITS * i + u + 1)
                            if e >= 2:
                                dve.wait_ge(down_ps, NE * i + e - 1)
                            nc.vector.tensor_tensor(hid[u % (2 * FC)], hid_a[u % RING], psum[:, 2 * (u % RING) + 1, :], ALU.mult).then_inc(hid_done, 1)
                        if e >= 1:
                            collect(e - 1)
                    collect(NE - 1)
                    for t in range(QT):
                        nc.vector.bn_stats(stats[:, t, :], acc[:, t, :])
                    dve.drain()
                    for t in range(QT):
                        last = nc.vector.bn_aggr(mv[:, t, :], stats[:, t, :])
                    last.then_inc(f_var, 1)
                    dve.wait_ge(f_std, i + 1)
                    nc.vector.reciprocal(rstd[:, :], std[:, :])
                    dve.drain()
                    for t in range(QT):
                        nc.vector.tensor_scalar(acc[:, t, :], acc[:, t, :], mv[:, t, 0:1], rstd[:, t:t + 1], ALU.subtract, ALU.mult)
                    dve.drain()
                    dve.wait_ge(x2t_in, 16 * QT * i + 16 * QT)
                    nc.vector.tensor_tensor(y_out, acc, x2_in, ALU.add).then_inc(y_done, 1)
                    dve.wait_ge(y_stored, 16 * QT * i + 16 * QT)


_INS = ['L0_attn_x', 'L0_attn_qkv_w', 'L0_attn_qkv_b', 'L0_attn_rpb', 'L0_attn_proj_w', 'L0_attn_proj_b',
        'L0_ffn_gru_w_ih', 'L0_ffn_gru_w_hh', 'L0_ffn_expr_w', 'L0_ffn_ctx_w', 'L0_ffn_ctx_b', 'L0_ffn_gate_w',
        'L0_ffn_up_w', 'L0_ffn_down_w', 'L0_ffn_shared_gate_w', 'L0_ffn_shared_up_w', 'L0_ffn_shared_down_w']
_OUTS = [((8, 512, 128), 'float32')]


def kernel(**inputs):
    import numpy as _np
    import concourse.bacc as _bacc
    from concourse import mybir as _mybir
    from concourse.bass_utils import run_bass_kernel_spmd as _run

    nc = _bacc.Bacc("TRN2", target_bir_lowering=False, num_devices=1)
    arrays, args = {}, []
    for name in _INS:
        a = _np.ascontiguousarray(inputs[name])
        arrays[f"in_{name}_dram"] = a
        args.append(nc.dram_tensor(f"in_{name}_dram", a.shape, _mybir.dt.from_np(a.dtype), kind="ExternalInput").ap())
    for i, (shape, dtype) in enumerate(_OUTS):
        dt = _mybir.dt.from_np(_np.dtype(dtype))
        args.append(nc.dram_tensor(f"out_{i}_dram", shape, dt, kind="ExternalOutput").ap())
    sandwich(nc, *args)
    r = _run(nc, [arrays], core_ids=[0])
    got = tuple(r.results[0][f"out_{i}_dram"] for i in range(len(_OUTS)))
    return got[0]
```

```python
from contextlib import ExitStack

import concourse.bass as bass
from concourse import mybir

F32 = mybir.dt.float32
F16 = mybir.dt.float16
U32 = mybir.dt.uint32
ALU = mybir.AluOpType
ACT = mybir.ActivationFunctionType
AX_X = mybir.AxisListType.X
RMAX = bass.bass_isa.ReduceOp.max
RADD = bass.bass_isa.ReduceOp.add

P = 128
BANK = 512


def sandwich(nc, x, qkv_w, qkv_b, rpb, proj_w, proj_b, w_ih, w_hh, expr_w, ctx_w, ctx_b,
             gate_w, up_w, down_w, sgate_w, sup_w, sdown_w, out):
    B, L, C = x.shape
    HEADS = rpb.shape[0]
    K = (rpb.shape[1] + 1) // 2
    NS = K // 2
    HD = C // HEADS
    QSCALE = float(HD) ** -0.5
    TOK = B * L
    TPS = L // P
    G = w_hh.shape[1]
    GM = G // P
    CH = GM
    NEXP = gate_w.shape[0]
    FF = gate_w.shape[1]
    FC = FF // P
    NE = NEXP + 1
    SP_T = P // B
    NT = TOK // P
    HALF = CH // 2
    WIN = K * HEADS
    EPS = 1e-5
    assert C == P and B * 4 == 32 and G == NEXP * P and GM == 8

    x2_dram = nc.dram_tensor("x2_scratch", (B, L, C), F32, kind="Internal").ap()
    hs_dram = nc.dram_tensor("hs_scratch", (L, P, CH * B), F32, kind="Internal").ap()

    ctx = ExitStack()
    with ctx:
        def sb(name, shape, dt=F32):
            return ctx.enter_context(nc.sbuf_tensor(name, shape, dt))

        def sem(name):
            return ctx.enter_context(nc.semaphore(name))

        psum = ctx.enter_context(nc.psum_tensor("psum", [P, 8, BANK], F32))

        room = sb("room", [P, GM * CH * 3 * P])
        taken = [0]

        def carve(*dims):
            n = 1
            for d in dims:
                n *= d
            a = room[:, taken[0]:taken[0] + n]
            taken[0] += n
            assert taken[0] <= GM * CH * 3 * P
            names = " ".join(f"d{i}" for i in range(len(dims)))
            return a if len(dims) == 1 else a.rearrange(
                f"p ({names}) -> p {names}", **{f"d{i}": d for i, d in enumerate(dims)})

        xs_room = sb("xs_room", [P, 2 * 3 * G])
        raw = [xs_room[:, i * 3 * G:(i + 1) * 3 * G] for i in range(2)]
        x_parts = xs_room[:, 0:(L + 2) * B].bitcast(F16).rearrange("p (t k) -> p t k", k=2 * B)
        xn2T = sb("xn2T", [P, TOK])
        w_ih_s = sb("w_ih_s", [P, 2, 4, 6, P], F16)
        w_hh_s = room[:, :].bitcast(F16).rearrange("p (s h k g r) -> p s h k g r", s=2, h=2, k=4 * CH, g=3)
        exprT = sb("exprT", [P, G])
        ctxT = sb("ctxT", [P, G])
        wqp = sb("wqp", [P, 4 * P])
        ident = sb("ident", [P, P])
        head_of = sb("head_of", [P, HEADS])
        spread = sb("spread", [P, P // HEADS, P])
        bias_win = sb("bias_win", [P, TPS, HEADS, K])
        proj_bias = sb("proj_bias", [P, C])
        qkv_bias = sb("qkv_bias", [P, 3])
        ctx_bias = sb("ctx_bias", [P, CH])
        eps = sb("eps", [P, 1])
        w_max = sb("w_max", [P, 3 * (GM + 1)])
        w_top = sb("w_top", [P, 1])
        w_all = sb("w_all", [P, 1])
        w_exp = sb("w_exp", [P, 1], U32)
        w_scale = sb("w_scale", [P, 1], U32)
        w_unscale = sb("w_unscale", [P, 1], U32)
        scale_f = w_scale[:, :].bitcast(F32)
        h_all = sb("h_all", [P, 1])
        h_exp = sb("h_exp", [P, 1], U32)
        h_scale = sb("h_scale", [P, 1], U32)
        h_unscale = sb("h_unscale", [P, 1], U32)
        h_scale_f = h_scale[:, :].bitcast(F32)
        h_unscale_f = h_unscale[:, :].bitcast(F32)
        unscale = sb("unscale", [P, 1])

        in_ready = sem("in_ready")
        bias_in = sem("bias_in")
        zeroed = sem("zeroed")
        consts = sem("consts")
        raw_in = [sem("raw_in0"), sem("raw_in1")]
        raw_tr = sem("raw_tr")
        raw_out = sem("raw_out")
        x_all = carve(NT, C)

        small = [(0, [(qkv_w, 3), (proj_w, 1)], wqp), (1, [(ctx_w, 8)], ctxT), (0, [(expr_w, 8)], exprT)]
        with nc.Block() as block:
            @block.sync
            def _(sp):
                for n, (q, parts, _) in enumerate(small):
                    if n >= 2:
                        sp.wait_ge(raw_tr, n - 1)
                    at = 0
                    for w, m in parts:
                        sp.dma_start(raw[q][:, at * P:(at + m) * P].rearrange("p (m k) -> p m k", m=m),
                                     w.rearrange("(m p) k -> p m k", p=P)).then_inc(raw_in[q], 16)
                        at += m
                for b in range(B):
                    sp.dma_start(x_all[:, b * TPS:(b + 1) * TPS, :],
                                 x[b].rearrange("(t p) c -> p t c", p=P)).then_inc(in_ready, 16)
                sp.dma_start(proj_bias[:, :], bass.AP(tensor=proj_b.tensor, offset=0, ap=[[0, P], [1, C]])).then_inc(in_ready, 16)
                sp.dma_start(qkv_bias[:, :], qkv_b.rearrange("(n p) -> p n", p=P),
                             allow_slow_non_contiguous=True).then_inc(in_ready, 16)
                sp.dma_start(ctx_bias[:, :], ctx_b.rearrange("(c p) -> p c", p=P),
                             allow_slow_non_contiguous=True).then_inc(in_ready, 16)
                for t in range(TPS):
                    lo, hi = (NS if t == 0 else 0), (P - NS if t == TPS - 1 else P)
                    sp.dma_start(bias_win[lo:hi, t, :, :],
                                 bass.AP(tensor=rpb.tensor, offset=NS, ap=[[0, hi - lo], [2 * K - 1, HEADS], [1, K]])
                                 ).then_inc(bias_in, 16)
                for n in range(NS):
                    for row, t, col in ((n, 0, 2 * NS - n), (P - NS + n, TPS - 1, NS - 1 - n)):
                        sp.dma_start(bias_win[row:row + 1, t, :, :], rpb[:, col:col + K].unsqueeze(0)).then_inc(bias_in, 16)
                sp.wait_ge(in_ready, 16 * (3 + B))

            @block.gpsimd
            def _(pool):
                nc.gpsimd.memset(ident[:, :], 0.0).then_inc(zeroed, 1)
                nc.gpsimd.memset(spread[:, :, :], 0.0).then_inc(zeroed, 1)
                nc.gpsimd.memset(head_of[:, :], 1.0).then_inc(zeroed, 1)
                nc.gpsimd.memset(eps[:, :], EPS)
                pool.wait_ge(zeroed, 3)
                nc.gpsimd.affine_select(out=ident[:, :], in_=ident[:, :], compare_op=ALU.not_equal, fill=1.0,
                                        base=0, pattern=[[-1, P]], channel_multiplier=1).then_inc(consts, 1)
                sv = spread[:, :, :].rearrange("p j (h d) -> p j h d", h=HEADS)
                nc.gpsimd.affine_select(out=sv, in_=sv, compare_op=ALU.not_equal, fill=1.0, base=0,
                                        pattern=[[-HEADS, P // HEADS], [-1, HEADS], [0, HD]],
                                        channel_multiplier=1).then_inc(consts, 1)
                nc.gpsimd.affine_select(out=head_of[:, :], in_=head_of[:, :], compare_op=ALU.is_ge, fill=0.0,
                                        base=0, pattern=[[-HD, HEADS]], channel_multiplier=1).then_inc(consts, 1)
                pool.wait_ge(consts, 3)
                nc.gpsimd.affine_select(out=head_of[:, :], in_=head_of[:, :], compare_op=ALU.is_ge, fill=0.0,
                                        base=HD - 1, pattern=[[HD, HEADS]], channel_multiplier=-1).then_inc(consts, 1)

            @block.tensor
            def _(pe):
                pe.wait_ge(consts, 1)
                landed = [0, 0]
                for n, (q, parts, _) in enumerate(small):
                    landed[q] += 16 * len(parts)
                    pe.wait_ge(raw_in[q], landed[q])
                    if n >= 2:
                        pe.wait_ge(raw_out, n - 1)
                    for m in range(sum(k for _, k in parts)):
                        last = nc.tensor.transpose(psum[:, 2 * q + m // 4, (m % 4) * P:(m % 4 + 1) * P],
                                                   raw[q][:, m * P:(m + 1) * P], ident[:, :])
                    last.then_inc(raw_tr, 1)

            @block.scalar
            def _(act):
                for n, (q, parts, dst) in enumerate(small):
                    act.wait_ge(raw_tr, n + 1)
                    for h in range(sum(k for _, k in parts) // 4):
                        last = nc.scalar.copy(dst[:, h * BANK:(h + 1) * BANK], psum[:, 2 * q + h, :])
                    last.then_inc(raw_out, 1)
                act.wait_ge(in_ready, 16 * (3 + B))
                nc.scalar.mul(qkv_bias[:, 0:1], qkv_bias[:, 0:1], QSCALE)

        att_prod = carve(K, L)
        pv_prod = carve(K, L)
        xn = carve(TPS, C)
        xn2 = carve(TPS, C)
        xnT = carve(L)
        qT, kT, vT = carve(L), carve(L), carve(L)
        scores = carve(TPS, K, HEADS)
        probs = carve(TPS, K, HEADS)
        pT = [carve(L), carve(L)]
        att = carve(TPS, C)
        x2 = carve(TPS, C)
        stats = sb("stats", [P, 3, TPS, 6])
        mv = sb("mv", [P, 3, TPS, 2])
        std = sb("std", [P, 3, TPS])
        rstd = sb("rstd", [P, 3, TPS])
        top = sb("top", [P, TPS, HEADS])
        total = sb("total", [P, TPS, HEADS])

        def window_ops(j):
            def tok_ends(a):
                w = a[:, 0:NS].unsqueeze(1)
                return bass.AP(tensor=w.tensor, offset=w.offset, ap=[w.ap[0], (L - NS, 2), (1, NS)])

            def key_ends(a):
                w = a[:, j:j + 1].unsqueeze(1)
                return bass.AP(tensor=w.tensor, offset=w.offset, ap=[w.ap[0], (L - K, 2), (0, NS)])
            return (lambda a: a[:, NS:L - NS], lambda a: a[:, j:j + L - 2 * NS]), (tok_ends, key_ends)

        pooled = [j for j in range(K) if j % 3 == 0]
        unpooled = [j for j in range(K) if j % 3]
        norm_var = [sem(f"norm_var{k}") for k in range(3)]
        norm_std = [sem(f"norm_std{k}") for k in range(3)]
        xn_done = sem("xn_done")
        xnT_ps = sem("xnT_ps")
        xnT_done = sem("xnT_done")
        qkv_ps = sem("qkv_ps")
        qkv_done = sem("qkv_done")
        qk_dve = sem("qk_dve")
        qk_pool = sem("qk_pool")
        score_ps = sem("score_ps")
        shifted = sem("shifted")
        exps = sem("exps")
        probs_done = sem("probs_done")
        pT_ps = sem("pT_ps")
        pT_done = sem("pT_done")
        spread_ps = sem("spread_ps")
        pv_done = sem("pv_done")
        proj_ps = sem("proj_ps")
        proj_read = sem("proj_read")
        x2_done = sem("x2_done")
        x2_stored = sem("x2_stored")
        xn2_done = sem("xn2_done")
        xn2T_ps = sem("xn2T_ps")
        xn2T_done = sem("xn2T_done")
        max_in = [sem("max_in0"), sem("max_in1")]
        max_read = sem("max_read")
        top_row = sem("top_row")
        top_all = sem("top_all")
        rec_in = [sem("rec_in0"), sem("rec_in1")]
        hh_rows = w_hh.rearrange("(g m p) k -> m p g k", g=3, p=P)
        ih_rows = w_ih.rearrange("(gm p) k -> p gm k", p=P)

        def load_hh(sp, q, m):
            return sp.dma_start(raw[q].rearrange("p (g k) -> p g k", g=3), hh_rows[bass.ds(m, 1)].rearrange("m p g k -> p (m g) k"))

        T_BANK, PROJ_BANK, PT_BANK = 3, 6, 7
        score_v = psum[:, 4:6, :].rearrange("p a (t w) -> p (a t) w", t=2)[:, :, 0:WIN]

        def norm_stats(dve, k, src):
            for t in range(TPS):
                nc.vector.bn_stats(stats[:, k, t, :], src(t))
            dve.drain()
            for t in range(TPS):
                last = nc.vector.bn_aggr(mv[:, k, t, :], stats[:, k, t, :])
            last.then_inc(norm_var[k], 1)

        def norm_apply(dve, k, n, src, dst):
            dve.wait_ge(norm_std[k], n)
            nc.vector.reciprocal(rstd[:, k, :], std[:, k, :])
            dve.drain()
            for t in range(TPS):
                last = nc.vector.tensor_scalar(dst(t), src(t), mv[:, k, t, 0:1], rstd[:, k, t:t + 1],
                                               ALU.subtract, ALU.mult)
            return last

        def present(s):
            return not isinstance(s, int) or 0 <= s < B

        def over_sequences(eng, step):
            for c in range(-3, 0):
                step(c)
            with eng.Fori(0, B - 3) as c:
                step(c)
            for c in range(B - 3, B):
                step(c)

        with nc.Block() as block:
            @block.sync
            def _(sp):
                for g in range(3):
                    sp.dma_start(raw[1][:, g * G:(g + 1) * G].rearrange("p (m k) -> p m k", k=C),
                                 ih_rows[:, g * GM:(g + 1) * GM, :]).then_inc(max_in[1], 16)
                load_hh(sp, 0, 0).then_inc(max_in[0], 16)

                def store(b):
                    sp.wait_ge(x2_done, b + 1)
                    sp.dma_start(x2_dram[bass.ds(b, 1)].rearrange("b (t p) c -> p (b t) c", p=P), x2).then_inc(x2_stored, 16)

                with sp.Fori(0, B - 1) as b:
                    store(b)
                    sp.wait_ge(max_read, b + 1)
                    load_hh(sp, 0, b + 1).then_inc(max_in[0], 16)
                sp.wait_ge(max_read, GM)
                load_hh(sp, 0, 0).then_inc(rec_in[0], 16)
                store(B - 1)

            @block.vector
            def _(dve):
                def step(c):
                    s, v = c + 2, c + 1
                    has_s, has_v, has_c = present(s), present(v), present(c)

                    def value_product(j):
                        if has_v:
                            dve.wait_ge(spread_ps, K * v + j + 1)
                            for p_of, v_of in window_ops(j):
                                last = nc.vector.tensor_tensor(p_of(pv_prod[:, j, :]), p_of(psum[:, j % 3, :]), v_of(vT), ALU.mult)
                            last.then_inc(pv_done, 1)

                    def key_product(j):
                        if has_s:
                            for q_of, k_of in window_ops(j):
                                last = nc.vector.tensor_tensor(q_of(att_prod[:, j, :]), q_of(qT), k_of(kT), ALU.mult)
                            last.then_inc(qk_dve, 1)

                    if has_c:
                        dve.wait_ge(proj_ps, c + 1)
                        nc.vector.tensor_tensor(att, psum[:, PROJ_BANK, :].rearrange("p (t c) -> p t c", t=TPS),
                                                proj_bias[:, :].unsqueeze(1).to_broadcast([P, TPS, C]),
                                                ALU.add).then_inc(proj_read, 1)
                    if has_v:
                        dve.wait_ge(qkv_done, 3 * v + 3)
                    value_product(0)
                    value_product(1)
                    if has_c:
                        dve.drain()
                        norm_stats(dve, 1, lambda t: att[:, t, :])
                    value_product(2)
                    if has_s:
                        dve.wait_ge(qkv_done, 3 * s + 2)
                    for n, j in enumerate(unpooled):
                        key_product(j)
                        if n % 2:
                            value_product(3 + n // 2)
                    if has_c:
                        norm_apply(dve, 1, c + 1, lambda t: att[:, t, :], lambda t: att[:, t, :])
                    value_product(7)
                    if has_c:
                        dve.drain()
                        nc.vector.tensor_tensor(x2, att, x_all[:, bass.ds(c * TPS, TPS), :], ALU.add).then_inc(x2_done, 1)
                    value_product(8)
                    if has_c:
                        dve.drain()
                        norm_stats(dve, 2, lambda t: x2[:, t, :])
                    if present(c + 3):
                        norm_stats(dve, 0, lambda t: x_all[:, bass.ds((c + 3) * TPS, TPS), :][:, t, :])
                    if has_s:
                        dve.wait_ge(score_ps, s + 1)
                        if not has_v:
                            dve.wait_ge(bias_in, 16 * (TPS + 2 * NS))
                        nc.vector.tensor_tensor(scores, score_v.rearrange("p t (k h) -> p t k h", h=HEADS),
                                                bias_win[:, :, :, :].rearrange("p t h k -> p t k h"), ALU.add)
                        dve.drain()
                        nc.vector.tensor_reduce(top[:, :, :], scores.rearrange("p t k h -> p t h k"), axis=AX_X, op=ALU.max)
                        dve.drain()
                        nc.vector.tensor_tensor(scores, scores, top[:, :, :].unsqueeze(2).to_broadcast([P, TPS, K, HEADS]),
                                                ALU.subtract).then_inc(shifted, 1)
                    value_product(9)
                    if has_c:
                        norm_apply(dve, 2, c + 1, lambda t: x2[:, t, :], lambda t: xn2[:, t, :]).then_inc(xn2_done, 1)
                    value_product(10)
                    if has_s:
                        dve.wait_ge(exps, s + 1)
                        nc.vector.tensor_reduce(total[:, :, :], probs.rearrange("p t k h -> p t h k"), axis=AX_X, op=ALU.add)
                        dve.drain()
                        nc.vector.reciprocal(total[:, :, :], total[:, :, :])
                        dve.drain()
                        nc.vector.tensor_tensor(probs, probs, total[:, :, :].unsqueeze(2).to_broadcast([P, TPS, K, HEADS]),
                                                ALU.mult).then_inc(probs_done, 1)
                    value_product(11)
                    value_product(12)
                    if present(c + 3):
                        if has_s:
                            dve.wait_ge(xnT_ps, s + 1)
                        norm_apply(dve, 0, c + 4, lambda t: x_all[:, bass.ds((c + 3) * TPS, TPS), :][:, t, :],
                                   lambda t: xn[:, t, :]).then_inc(xn_done, 1)
                    if has_c:
                        dve.wait_ge(max_in[0], 16 * c + 16)
                        magnitude(0, 3 * c).then_inc(max_read, 1)
                        dve.wait_ge(x2_stored, 16 * c + 16)
                        dve.wait_ge(xn2T_ps, c + 1)

                def magnitude(q, at):
                    for g in range(3):
                        last = nc.vector.tensor_reduce(w_max[:, bass.ds(at + g, 1)], raw[q][:, g * G:(g + 1) * G], axis=AX_X,
                                                       op=ALU.max, apply_absolute_value=True)
                    return last

                over_sequences(dve, step)
                dve.wait_ge(max_in[1], 48)
                magnitude(1, 3 * GM)
                dve.drain()
                nc.vector.tensor_reduce(w_top[:, :], w_max[:, :], axis=AX_X, op=ALU.max).then_inc(top_row, 1)
                dve.wait_ge(top_all, 1)
                nc.vector.tensor_scalar(w_all[:, :], w_all[:, :], 2.0 ** -100, None, ALU.max)
                dve.drain()
                nc.vector.tensor_scalar(w_exp[:, :], w_all[:, :].bitcast(U32), 0x7F800000, None, ALU.bitwise_and)
                dve.drain()
                nc.vector.tensor_scalar(w_scale[:, :], w_exp[:, :], -1.0, float(268 << 23), ALU.mult, ALU.add)
                nc.vector.tensor_scalar(w_unscale[:, :], w_exp[:, :], float(14 << 23), None, ALU.subtract)

            @block.gpsimd
            def _(pool):
                with pool.Fori(0, B) as b:
                    pool.wait_ge(qkv_done, 3 * b + 2)
                    for j in pooled:
                        for q_of, k_of in window_ops(j):
                            last = nc.gpsimd.tensor_tensor(q_of(att_prod[:, j, :]), q_of(qT), k_of(kT), ALU.mult)
                        last.then_inc(qk_pool, 1)
                pool.wait_ge(top_row, 1)
                nc.gpsimd.partition_all_reduce(w_all[:, :], w_top[:, :], P, RMAX).then_inc(top_all, 1)

            @block.scalar
            def _(act):
                def roots(k, n):
                    act.wait_ge(norm_var[k], n)
                    nc.scalar.activation(std[:, k, :], mv[:, k, :, 1], ACT.Sqrt, bias=eps[:, 0:1]).then_inc(norm_std[k], 1)

                def step(c):
                    s = c + 2

                    def projected(n, dst):
                        act.wait_ge(qkv_ps, 3 * s + n + 1)
                        nc.scalar.activation(dst, psum[:, T_BANK, :], ACT.Identity, scale=QSCALE if n == 0 else 1.0,
                                             bias=qkv_bias[:, n:n + 1]).then_inc(qkv_done, 1)

                    if present(s):
                        act.wait_ge(xnT_ps, s + 1)
                        nc.scalar.copy(xnT, psum[:, T_BANK, :]).then_inc(xnT_done, 1)
                        projected(0, qT)
                        projected(1, kT)
                    if present(c):
                        roots(1, c + 1)
                        roots(2, c + 1)
                    if present(c + 3):
                        roots(0, c + 4)
                    if present(s):
                        act.wait_ge(shifted, s + 1)
                        nc.scalar.activation(probs, scores, ACT.Exp).then_inc(exps, 1)
                    if present(c):
                        act.wait_ge(xn2T_ps, c + 1)
                        dst = xn2T[:, :].rearrange("p (t b) -> p t b", b=B)[:, :, bass.ds(c, 1)]
                        nc.scalar.copy(dst, psum[:, T_BANK, :].unsqueeze(2)).then_inc(xn2T_done, 1)
                    if present(s):
                        act.wait_ge(pT_ps, s + 1)
                        nc.scalar.copy(pT[0], psum[:, PT_BANK, :])
                        nc.scalar.copy(pT[1][0:WIN - P, :], psum[0:WIN - P, T_BANK, :]).then_inc(pT_done, 1)
                        projected(2, vT)

                over_sequences(act, step)

            @block.tensor
            def _(pe):
                def step(c):
                    s, v = c + 2, c + 1
                    has_s, has_v = present(s), present(v)

                    def project_in(n):
                        if has_s:
                            nc.tensor.matmul(psum[:, T_BANK, :], wqp[:, n * P:(n + 1) * P], xnT,
                                             start=True, stop=True).then_inc(qkv_ps, 1)

                    def score(j):
                        if j in pooled:
                            pe.wait_ge(qk_pool, len(pooled) * s + pooled.index(j) + 1)
                        else:
                            pe.wait_ge(qk_dve, len(unpooled) * s + unpooled.index(j) + 1)
                        for t in range(TPS):
                            last = nc.tensor.matmul(score_v[:, t, j * HEADS:(j + 1) * HEADS],
                                                    att_prod[:, j, t * P:(t + 1) * P], head_of[:, :],
                                                    start=True, stop=True)
                        if j == K - 1:
                            last.then_inc(score_ps, 1)

                    def spread_key(j):
                        if has_v:
                            half, rows = (0, P) if j < P // HEADS else (1, WIN - P)
                            nc.tensor.matmul(psum[:, j % 3, :], spread[0:rows, j % (P // HEADS), :], pT[half][0:rows, :],
                                             start=True, stop=True).then_inc(spread_ps, 1)

                    def project(j):
                        if has_v:
                            pe.wait_ge(pv_done, K * v + j + 1)
                            if j == 0 and present(c):
                                pe.wait_ge(proj_read, c + 1)
                            for t in range(TPS):
                                last = nc.tensor.matmul(psum[:, PROJ_BANK, t * P:(t + 1) * P], pv_prod[:, j, t * P:(t + 1) * P],
                                                        wqp[:, 3 * P:4 * P], start=(j == 0 and t == 0), stop=(j == K - 1),
                                                        skip_group_check=True)
                            if j == K - 1:
                                last.then_inc(proj_ps, 1)

                    if has_v:
                        pe.wait_ge(pT_done, v + 1)
                    spread_key(0)
                    if has_s:
                        pe.wait_ge(xn_done, s + 1)
                        if has_v:
                            pe.wait_ge(qkv_done, 3 * v + 3)
                        for t in range(TPS):
                            last = nc.tensor.transpose(psum[:, T_BANK, t * P:(t + 1) * P], xn[:, t, :], ident[:, :])
                        last.then_inc(xnT_ps, 1)
                    spread_key(1)
                    if has_s:
                        pe.wait_ge(xnT_done, s + 1)
                    project_in(0)
                    spread_key(2)
                    if has_s:
                        pe.wait_ge(qkv_done, 3 * s + 1)
                    project_in(1)
                    scored = 0
                    for j in range(K - 3):
                        project(j)
                        spread_key(j + 3)
                        upto = min(K, max(0, (K * j + 5) // 6))
                        if has_s:
                            for k in range(scored, upto):
                                score(k)
                        scored = upto
                    if present(c):
                        pe.wait_ge(xn2_done, c + 1)
                        if has_s:
                            pe.wait_ge(qkv_done, 3 * s + 2)
                        for t in range(TPS):
                            last = nc.tensor.transpose(psum[:, T_BANK, t * P:(t + 1) * P], xn2[:, t, :], ident[:, :])
                        last.then_inc(xn2T_ps, 1)
                    project(10)
                    if has_s:
                        pe.wait_ge(probs_done, s + 1)
                        if present(c):
                            pe.wait_ge(xn2T_done, c + 1)
                        else:
                            pe.wait_ge(qkv_done, 3 * s + 2)
                        for t in range(TPS):
                            row = probs[:, t, :, :].rearrange("p k h -> p (k h)")
                            nc.tensor.transpose(psum[:, PT_BANK, t * P:(t + 1) * P], row[:, 0:P], ident[:, :])
                            last = nc.tensor.transpose(psum[0:WIN - P, T_BANK, t * P:(t + 1) * P], row[:, P:WIN], ident[:, :])
                        last.then_inc(pT_ps, 1)
                    project(11)
                    project(12)
                    if has_s:
                        pe.wait_ge(pT_done, s + 1)
                    project_in(2)

                over_sequences(pe, step)

        rec_tr = sem("rec_tr")
        rec_hi = sem("rec_hi")
        rec_lo = sem("rec_lo")

        def ih_place(g, h):
            return h if g == 2 else 2 + 2 * h + g

        with nc.Block() as block:
            @block.sync
            def _(sp):
                with sp.Fori(0, GM // 2 - 1) as i:
                    sp.wait_ge(rec_tr, 6 * i + 3)
                    load_hh(sp, 1, i + HALF).then_inc(rec_in[1], 16)
                    sp.wait_ge(rec_tr, 6 * i + 6)
                    load_hh(sp, 0, i + 1).then_inc(rec_in[0], 16)
                sp.wait_ge(rec_tr, 3 * GM - 3)
                load_hh(sp, 1, GM - 1).then_inc(rec_in[1], 16)

            def by_group(g, m):
                return psum[:, 2 * g + m // 4, :].rearrange("p (j c u) -> p c j u", j=4, u=32)[:, m % 4]

            def banks(g):
                return psum[:, 2 * g:2 * g + 2, :].rearrange("p a (c r) -> p (a c) r", r=P)

            def in_groups(g):
                return psum[:, 2 * g:2 * g + 2, :].rearrange("p a (k u) -> p (a k) u", u=32)

            def halves(g, h):
                return psum[:, 2 * g + h, :].rearrange("p (j r) -> p j r", j=4)

            @block.tensor
            def _(pe):
                for g in range(3):
                    for m in range(GM):
                        last = nc.tensor.transpose(by_group(g, m), raw[1][:, (g * GM + m) * P:(g * GM + m + 1) * P], ident[:, :])
                    last.then_inc(rec_tr, 1)
                with pe.Fori(0, GM // 2) as i:
                    for q in range(2):
                        pe.wait_ge(rec_in[q], 16 * i + 16)
                        for g in range(3):
                            pe.wait_ge(rec_lo, 6 * i + 3 * q + g + 1)
                            for c in range(CH):
                                last = nc.tensor.transpose(banks(g)[:, c, :], raw[q][:, g * G + c * P:g * G + (c + 1) * P], ident[:, :])
                            last.then_inc(rec_tr, 1)

            @block.scalar
            def _(act):
                for g in range(3):
                    act.wait_ge(rec_tr, g + 1)
                    for h in range(2):
                        last = nc.scalar.activation(w_ih_s[:, 0, :, ih_place(g, h), :], halves(g, h), ACT.Copy, scale=scale_f[:, 0:1])
                    last.then_inc(rec_hi, 1)
                with act.Fori(0, GM // 2) as i:
                    for q in range(2):
                        for g in range(3):
                            act.wait_ge(rec_tr, 6 * i + 3 * q + g + 4)
                            nc.scalar.activation(w_hh_s[:, 0, q, :, g, bass.ds(i * 32, 32)],
                                                 in_groups(g), ACT.Copy, scale=scale_f[:, 0:1]).then_inc(rec_hi, 1)

            @block.vector
            def _(dve):
                for g in range(3):
                    dve.wait_ge(rec_hi, g + 1)
                    for h in range(2):
                        last = nc.vector.scalar_tensor_tensor(w_ih_s[:, 1, :, ih_place(g, h), :], halves(g, h), scale_f[:, 0:1],
                                                              w_ih_s[:, 0, :, ih_place(g, h), :], ALU.mult, ALU.subtract)
                    last.then_inc(rec_lo, 1)
                with dve.Fori(0, GM // 2) as i:
                    for q in range(2):
                        for g in range(3):
                            dve.wait_ge(rec_hi, 6 * i + 3 * q + g + 4)
                            hi, lo = (w_hh_s[:, s, q, :, g, bass.ds(i * 32, 32)] for s in range(2))
                            nc.vector.scalar_tensor_tensor(lo, in_groups(g), scale_f[:, 0:1], hi,
                                                           ALU.mult, ALU.subtract).then_inc(rec_lo, 1)

        HB = HALF * B
        NSHIFT = NEXP // 2 + 1
        WRAP = NEXP + NSHIFT - 1
        h_parts = sb("h_parts", [P, 2, CH, 4 * B], F16)
        x_now = sb("x_now", [P, 4 * B], F16)
        h_full = sb("h_full", [P, 2, CH * B])
        turned = sb("turned", [P, 2, 3, P])
        gates = sb("gates", [P, 2, 3, HB])
        xn_turned = sb("xn_turned", [P, 2 * P])
        xn_pair = sb("xn_pair", [P, CH, 2, B])
        neg_h_scale = sb("neg_h_scale", [P, 1])
        rz = sb("rz", [P, 2, 2, HB])
        pre_n = sb("pre_n", [P, 2, 2, HB])
        n_act = sb("n_act", [P, 2, HB])
        keep = sb("keep", [P, 2, HB])
        not_z = sb("not_z", [P, 2, HB])
        fresh = sb("fresh", [P, 2, HB])
        x_mean = sb("x_mean", [P, B])
        history = sb("history", [P, CH, 2, SP_T, B], F16)
        ident_16 = sb("ident_16", [P, P], F16)
        x_tile = sb("x_tile", [P, P])
        routes = sb("routes", [P, 2, WRAP, P])
        products = sb("products", [P, NSHIFT, P])
        gram = sb("gram", [P, NT + 1, NEXP, NSHIFT + 2])
        xn_ps = sem("xn_ps")
        xn_read = sem("xn_read")
        xn_ready = sem("xn_ready")
        mean_done = sem("mean_done")
        h0_ps = sem("h0_ps")
        h0_top = sem("h0_top")
        h0_all = sem("h0_all")
        h_scaled = sem("h_scaled")
        x_first = sem("x_first")
        cleared = sem("cleared")
        x_staged = sem("x_staged")
        x_used = sem("x_used")

        def two(name):
            return [sem(name + "A"), sem(name + "B")]

        h_ready, bank_free, gates_ps = two("h_ready"), two("bank_free"), two("gates_ps")
        rz_turned, gates_in, n_in, rz_done = two("rz_turned"), two("gates_in"), two("n_in"), two("rz_done")
        hn_scaled, pre_done, n_done, keep_done = two("hn_scaled"), two("pre_done"), two("n_done"), two("keep_done")
        fresh_done, first_part = two("fresh_done"), two("first_part")
        kept = sem("kept")
        tile_ps = sem("tile_ps")
        tile_read = sem("tile_read")
        tile_staged = sem("tile_staged")
        multiplied = sem("multiplied")
        dots_half = sem("dots_half")
        dots_done = sem("dots_done")

        def part(parts, i):
            return parts[:, :, i * B:(i + 1) * B]

        def by_chunk(a):
            return a.rearrange("p (c b) -> p c b", b=B)

        def tile_products(pe):
            for c in range(CH):
                for s in range(2):
                    nc.tensor.matmul(psum[:, 4 + c // 4, (c % 4) * P:(c % 4 + 1) * P],
                                     history[:, c, s, :, :].rearrange("p t b -> p (t b)"), ident_16[:, :],
                                     start=(s == 0), stop=(s == 1))
            for h in range(2):
                last = nc.tensor.matmul(psum[:, 6 + h, :], x_tile[:, :], exprT[:, h * BANK:(h + 1) * BANK], start=True, stop=True)
            return last

        def tile_copies(act):
            for lo, bank in ((0, 4), (4, 5), (NEXP, 4)):
                nc.scalar.activation(routes[:, 0, lo:lo + 4, :].rearrange("p e d -> p (e d)"), psum[:, bank, :],
                                     ACT.Copy, scale=h_unscale_f[:, 0:1])
            for h in range(2):
                last = nc.scalar.copy(routes[:, 1, 4 * h:4 * h + 4, :].rearrange("p e d -> p (e d)"), psum[:, 6 + h, :])
            return last

        def expr_dots(e):
            here = routes[:, :, bass.ds(e, 1), :].rearrange("p a e d -> p a (e d)")
            return nc.vector.tensor_tensor(products[:, 0:2, :], here, routes[:, 1, bass.ds(e, 1), :].to_broadcast([P, 2, P]), ALU.mult)

        def state_dots(e):
            return nc.vector.tensor_tensor(products[:, :, :], routes[:, 0, bass.ds(e, 1), :].to_broadcast([P, NSHIFT, P]),
                                           routes[:, 0, bass.ds(e, NSHIFT), :], ALU.mult)

        def sum_dots(slot, e, lo, n):
            dst = gram[:, bass.ds(slot, 1), bass.ds(e, 1), lo:lo + n].rearrange("p a e s -> p (a e s)")
            return nc.vector.tensor_reduce(dst, products[:, 0:n, :], axis=AX_X, op=ALU.add)

        def tokens(i):
            return xn2T[:, i * TOK // 4:(i + 1) * TOK // 4].rearrange("p (t b) -> p t b", b=B)

        def token_part(i, k):
            return x_parts[:, i * L // 4:(i + 1) * L // 4, k * B:(k + 1) * B]

        with nc.Block() as block:
            @block.gpsimd
            def _(pool):
                nc.gpsimd.memset(h_parts[:, :, :, :], 0.0).then_inc(cleared, 1)
                nc.gpsimd.memset(x_parts[:, L + 1, :], 0.0)
                nc.gpsimd.memset(x_parts[:, L, :], 0.0)
                nc.gpsimd.memset(history[:, :, :, :, :], 0.0)
                nc.gpsimd.memset(x_tile[:, :], 0.0)
                nc.gpsimd.tensor_copy(ident_16[:, :], ident[:, :])
                pool.wait_ge(h0_top, 1)
                nc.gpsimd.partition_all_reduce(h_all[:, :], w_top[:, :], P, RMAX).then_inc(h0_all, 1)

            @block.scalar
            def _(act):
                act.wait_ge(h_scaled, 1)
                for i in range(4):
                    nc.scalar.activation(token_part(i, 0), tokens(i), ACT.Copy, scale=h_scale_f[:, 0:1]).then_inc(x_first, 1)

            @block.vector
            def _(dve):
                nc.vector.tensor_reduce(x_mean[:, :], xn2T[:, :].rearrange("p (t b) -> p b t", b=B), axis=AX_X, op=ALU.add)
                dve.drain()
                nc.vector.tensor_scalar(x_mean[:, :], x_mean[:, :], 1.0 / L, None, ALU.mult).then_inc(mean_done, 1)
                dve.wait_ge(h0_ps, 1)
                dve.wait_ge(cleared, 1)
                full = by_chunk(h_full[:, 0, :])
                nc.vector.tensor_tensor(full, by_chunk(psum[:, 0, 0:CH * B]),
                                        ctx_bias[:, :].unsqueeze(2).to_broadcast([P, CH, B]), ALU.add)
                dve.drain()
                nc.vector.tensor_reduce(w_top[:, :], h_full[:, 0, :], axis=AX_X, op=ALU.max,
                                        apply_absolute_value=True).then_inc(h0_top, 1)
                dve.wait_ge(h0_all, 1)
                nc.vector.tensor_scalar(h_all[:, :], h_all[:, :], 1.0, None, ALU.max)
                dve.drain()
                nc.vector.tensor_scalar(h_exp[:, :], h_all[:, :].bitcast(U32), 0x7F800000, None, ALU.bitwise_and)
                dve.drain()
                nc.vector.tensor_scalar(h_scale[:, :], h_exp[:, :], -1.0, float(266 << 23), ALU.mult, ALU.add)
                nc.vector.tensor_scalar(h_unscale[:, :], h_exp[:, :], float(12 << 23), None, ALU.subtract)
                dve.drain().then_inc(h_scaled, 1)
                nc.vector.tensor_scalar(neg_h_scale[:, :], h_scale_f, -1.0, None, ALU.mult)
                nc.vector.tensor_tensor(unscale[:, :], w_unscale[:, :].bitcast(F32), h_unscale_f, ALU.mult)
                nc.vector.tensor_scalar(h_full[:, 0, :], h_full[:, 0, :], h_scale_f[:, 0:1], None, ALU.mult)
                dve.drain()
                nc.vector.tensor_copy(part(h_parts[:, 0, :, :], 0), full)
                dve.drain()
                nc.vector.tensor_tensor(part(h_parts[:, 0, :, :], 1), full, part(h_parts[:, 0, :, :], 0), ALU.subtract)
                for i in range(4):
                    dve.wait_ge(x_first, i + 1)
                    nc.vector.scalar_tensor_tensor(token_part(i, 1), tokens(i), h_scale_f[:, 0:1], token_part(i, 0),
                                                   ALU.mult, ALU.subtract)
                dve.drain()
                for half in range(2):
                    dve.sem_inc(h_ready[half], 1)
                    dve.sem_inc(bank_free[half], 1)
                dve.sem_inc(kept, 2)
                dve.sem_inc(tile_staged, 1)
                dve.sem_inc(tile_read, 1)
                dve.sem_inc(dots_done, 1)

            @block.tensor
            def _(pe):
                pe.wait_ge(mean_done, 1)
                for c in range(CH):
                    last = nc.tensor.matmul(psum[:, 0, c * B:(c + 1) * B], ctxT[:, c * P:(c + 1) * P], x_mean[:, :], start=True, stop=True)
                last.then_inc(h0_ps, 1)

        with nc.Block() as block:
            PAIRS = SP_T // 2
            XN_BANK = 2
            EARLY = 2

            def over_steps(eng, body):
                with eng.Fori(0, NT) as n:
                    body(n, 0, True)
                    with eng.Fori(1, PAIRS) as i:
                        body(n, i, False)

            @block.gpsimd
            def _(pool):
                nc.gpsimd.tensor_copy(x_now[:, :], x_parts[:, 0:2, :].rearrange("p t k -> p (t k)")).then_inc(x_staged, 1)

                def pair(n, i, first):
                    t0 = n * SP_T + 2 * i
                    pool.wait_ge(x_used, n * PAIRS + i + 1)
                    nc.gpsimd.tensor_copy(x_now[:, :].rearrange("p (t k) -> p t k", t=2), x_parts[:, bass.ds(t0 + 2, 2), :]).then_inc(x_staged, 1)
                    for q in range(2):
                        for half in range(2):
                            pool.wait_ge(rz_done[half], t0 + q + 1)
                            nc.gpsimd.tensor_tensor(keep[:, half, :], rz[:, half, 1, :], h_full[:, q, half * HB:(half + 1) * HB], ALU.mult)
                            nc.gpsimd.tensor_scalar(not_z[:, half, :], rz[:, half, 1, :], neg_h_scale[:, 0:1], h_scale_f[:, 0:1], ALU.mult, ALU.add).then_inc(keep_done[half], 1)
                    if first:
                        nc.gpsimd.tensor_copy(x_tile[:, :], xn2T[:, bass.ds(n * P, P)]).then_inc(tile_staged, 1)

                over_steps(pool, pair)

            @block.tensor
            def _(pe):
                def state_share(q, half, chunks):
                    for c in chunks:
                        for s in range(2):
                            for j in range(4):
                                last = nc.tensor.matmul(psum[32 * j:32 * j + 32, half, 0:3 * P], h_parts[:, q, c, :],
                                                        w_hh_s[:, s, half, 4 * c + j, :, :].rearrange("p g r -> p (g r)"),
                                                        start=False, stop=(c == CH - 1 and s == 1), skip_group_check=True)
                    return last

                def token_products(columns, place):
                    for s in range(2):
                        for j in range(4):
                            last = nc.tensor.matmul(psum[32 * j:32 * j + 32, columns, 0:2 * P], x_now[:, :],
                                                    w_ih_s[:, s, j, place:place + 2, :].rearrange("p g r -> p (g r)"),
                                                    start=(s == 0), stop=False, skip_group_check=True)
                    return last

                def token_share(half):
                    return token_products(half, 2 + 2 * half)

                def token_n():
                    token_products(XN_BANK, 0).then_inc(xn_ps, 1)

                pe.wait_ge(x_staged, 1)
                token_n()

                def pair(n, i, first):
                    t0 = n * SP_T + 2 * i
                    for q in range(2):
                        t1 = t0 + q + 1
                        if q == 0:
                            pe.wait_ge(bank_free[0], t1)
                            token_share(0)
                        else:
                            pe.wait_ge(x_staged, n * PAIRS + i + 2)
                            pe.wait_ge(xn_read, n * PAIRS + i + 1)
                            token_n()
                        pe.wait_ge(h_ready[0], t1)
                        state_share(q, 0, range(0, HALF))
                        pe.wait_ge(bank_free[1], t1)
                        if q == 0:
                            token_share(1).then_inc(x_used, 1)
                        state_share(q, 1, range(0, EARLY))
                        pe.wait_ge(h_ready[1], t1)
                        state_share(q, 0, range(HALF, CH)).then_inc(gates_ps[0], 1)
                        state_share(q, 1, range(EARLY, CH)).then_inc(gates_ps[1], 1)
                        if first and q == 0:
                            pe.wait_ge(kept, n * SP_T + 2)
                            pe.wait_ge(tile_staged, n + 1)
                            pe.wait_ge(tile_read, n + 1)
                            tile_products(pe).then_inc(tile_ps, 1)

                over_steps(pe, pair)

            @block.vector
            def _(dve):
                def summed(q, half, g, n):
                    by_part = turned[:, half, g:g + n, :].rearrange("p g (k s b) -> p (g k) s b", s=4, b=B)
                    return nc.vector.tensor_tensor(by_chunk(gates[:, half, g:g + n, :].rearrange("p g k -> p (g k)")),
                                                   by_part[:, :, 2 * q, :], by_part[:, :, 2 * q + 1, :], ALU.add)

                def turn_xn(pairs):
                    dve.wait_ge(xn_ps, pairs)
                    nc.vector.transpose(xn_turned[:, :], psum[:, XN_BANK, 0:2 * P]).then_inc(xn_read, 1)
                    dve.wait_ge(xn_read, pairs)
                    by_part = xn_turned[:, :].rearrange("p (k q s b) -> p k q s b", q=2, s=2, b=B)
                    nc.vector.tensor_tensor(xn_pair[:, :, :, :], by_part[:, :, :, 0, :], by_part[:, :, :, 1, :],
                                            ALU.add).then_inc(xn_ready, 1)

                def turn(t1, q, half):
                    bank = psum[:, half, 0:3 * P].rearrange("p (g r) -> p g r", g=3)
                    dve.wait_ge(gates_ps[half], t1)
                    if half == 0:
                        dve.wait_ge(kept, t1)
                    nc.vector.transpose(turned[:, half, 0:2, :], bank[:, 0:2, :]).then_inc(rz_turned[half], 1)
                    nc.vector.transpose(turned[:, half, 2:3, :], bank[:, 2:3, :]).then_inc(bank_free[half], 1)

                def before_tanh(t1, q, half):
                    dve.wait_ge(rz_turned[half], t1)
                    summed(q, half, 0, 2).then_inc(gates_in[half], 1)
                    dve.wait_ge(bank_free[half], t1 + 1)
                    summed(q, half, 2, 1).then_inc(n_in[half], 1)
                    dve.wait_ge(rz_done[half], t1)
                    dve.wait_ge(n_in[half], t1)
                    nc.vector.tensor_tensor(pre_n[:, half, 0, :], rz[:, half, 0, :], gates[:, half, 2, :], ALU.mult).then_inc(hn_scaled[half], 1)
                    dve.wait_ge(hn_scaled[half], t1)
                    nc.vector.tensor_tensor(by_chunk(pre_n[:, half, 1, :]), by_chunk(pre_n[:, half, 0, :]),
                                            xn_pair[:, half * HALF:(half + 1) * HALF, q, :], ALU.add).then_inc(pre_done[half], 1)

                def after_tanh(t1, q, half):
                    dve.wait_ge(n_done[half], t1)
                    dve.wait_ge(keep_done[half], t1)
                    full = h_full[:, 1 - q, half * HB:(half + 1) * HB]
                    parts = h_parts[:, 1 - q, half * HALF:(half + 1) * HALF, :]
                    nc.vector.tensor_tensor(fresh[:, half, :], n_act[:, half, :], not_z[:, half, :], ALU.mult).then_inc(fresh_done[half], 1)
                    dve.wait_ge(fresh_done[half], t1)
                    nc.vector.tensor_tensor(part(parts, 2 * (1 - q)), by_chunk(fresh[:, half, :]), by_chunk(keep[:, half, :]), ALU.add)
                    nc.vector.tensor_tensor(full, fresh[:, half, :], keep[:, half, :], ALU.add).then_inc(first_part[half], 1)
                    dve.wait_ge(first_part[half], t1)
                    nc.vector.tensor_tensor(part(parts, 2 * (1 - q) + 1), by_chunk(full), part(parts, 2 * (1 - q)), ALU.subtract).then_inc(h_ready[half], 1)

                def pair(n, i, first):
                    t0 = n * SP_T + 2 * i
                    for q in range(2):
                        t1 = t0 + q + 1
                        turn(t1, q, 0)
                        before_tanh(t1, q, 0)
                        after_tanh(t1, q, 0)
                        turn(t1, q, 1)
                        before_tanh(t1, q, 1)
                        after_tanh(t1, q, 1)
                        if q == 0:
                            dve.wait_ge(tile_read, n + 2)
                            state_dots(i).then_inc(multiplied, 1)
                            dve.wait_ge(multiplied, t0 + 1)
                            sum_dots(n, i, 0, NSHIFT).then_inc(dots_half, 1)
                        else:
                            turn_xn(n * PAIRS + i + 2)
                            dve.wait_ge(dots_half, n * PAIRS + i + 1)
                            expr_dots(i).then_inc(multiplied, 1)
                            dve.wait_ge(xn_ready, n * PAIRS + i + 2)
                            dve.wait_ge(multiplied, t0 + 2)
                            sum_dots(n, i, NSHIFT, 2).then_inc(dots_done, 1)

                turn_xn(1)
                dve.wait_ge(xn_ready, 1)
                over_steps(dve, pair)

            @block.scalar
            def _(act):
                def pair(n, i, first):
                    t0 = n * SP_T + 2 * i
                    for q in range(2):
                        t1 = t0 + q + 1
                        for half in range(2):
                            act.wait_ge(gates_in[half], t1)
                            nc.scalar.activation(rz[:, half, :, :], gates[:, half, 0:2, :], ACT.Sigmoid,
                                                 scale=unscale[:, 0:1]).then_inc(rz_done[half], 1)
                            act.wait_ge(pre_done[half], t1)
                            nc.scalar.activation(n_act[:, half, :], pre_n[:, half, 1, :], ACT.Tanh,
                                                 scale=unscale[:, 0:1]).then_inc(n_done[half], 1)
                        act.wait_ge(h_ready[1], t1 + 1)
                        act.wait_ge(tile_ps, n + 1)
                        nc.scalar.copy(history[:, :, :, bass.ds(2 * i + q, 1), :].rearrange("p c s t b -> p c s (t b)"),
                                       h_parts[:, 1 - q, :, 2 * (1 - q) * B:2 * (2 - q) * B].rearrange("p c (s b) -> p c s b", b=B)
                                       ).then_inc(kept, 1)
                        if first and q == 0:
                            act.wait_ge(dots_done, n * PAIRS + 1)
                            tile_copies(act).then_inc(tile_read, 1)

                over_steps(act, pair)

        taken[0] = 0
        expT = carve(NE, 6, P)
        mix = carve(NT, NEXP)
        ew_in = [sem("ew_in0"), sem("ew_in1")]
        ew_tr = sem("ew_tr")
        ew_out = sem("ew_out")
        last_ps = sem("last_ps")
        last_read = sem("last_read")
        loads = []
        for kind, (w, sw) in enumerate(((gate_w, sgate_w), (up_w, sup_w), (down_w, sdown_w))):
            for lo in range(0, NEXP, 4):
                loads.append((kind, lo, 4, w[lo:lo + 4]))
            loads.append((kind, NEXP, 1, sw.unsqueeze(0)))

        with nc.Block() as block:
            @block.sync
            def _(sp):
                for n, (kind, lo, ne, w) in enumerate(loads):
                    if n >= 2:
                        sp.wait_ge(ew_tr, n - 1)
                    if kind < 2:
                        sp.dma_start(raw[n % 2][:, 0:2 * ne * P].rearrange("p (e k) -> p e k", k=P), w.rearrange("e (f p) k -> p (e f) k", p=P)).then_inc(ew_in[n % 2], 16)
                    else:
                        sp.dma_start(raw[n % 2][:, 0:2 * ne * P].rearrange("p (e k) -> p e k", k=FF), w.rearrange("e p k -> p e k")).then_inc(ew_in[n % 2], 16)

            @block.tensor
            def _(pe):
                tile_products(pe).then_inc(last_ps, 1)
                for n, (kind, lo, ne, w) in enumerate(loads):
                    pe.wait_ge(ew_in[n % 2], 16 * (n // 2 + 1))
                    if n >= 2:
                        pe.wait_ge(ew_out, n - 1)
                    for m in range(2 * ne):
                        last = nc.tensor.transpose(psum[:, 2 * (n % 2) + m // 4, (m % 4) * P:(m % 4 + 1) * P],
                                                   raw[n % 2][:, m * P:(m + 1) * P], ident[:, :])
                    last.then_inc(ew_tr, 1)

            @block.scalar
            def _(act):
                act.wait_ge(last_ps, 1)
                tile_copies(act).then_inc(last_read, 1)
                for n, (kind, lo, ne, w) in enumerate(loads):
                    act.wait_ge(ew_tr, n + 1)
                    for h in range((ne + 1) // 2):
                        k = min(2, ne - 2 * h)
                        last = nc.scalar.copy(expT[:, lo + 2 * h:lo + 2 * h + k, 2 * kind:2 * kind + 2, :],
                                              psum[:, 2 * (n % 2) + h, 0:2 * k * P].rearrange("p (e f r) -> p e f r", e=k, f=2))
                    last.then_inc(ew_out, 1)

            @block.vector
            def _(dve):
                dve.wait_ge(last_read, 1)
                for e in range(NEXP):
                    expr_dots(e)
                    dve.drain()
                    sum_dots(NT, e, NSHIFT, 2)
                    dve.drain()
                    state_dots(e)
                    dve.drain()
                    sum_dots(NT, e, 0, NSHIFT)
                    dve.drain()

        dots = gram[:, 1:NT + 1, :, :]
        wrap = NEXP // 2

        def wide(name, n=NEXP):
            return carve(NT, n)
        length = wide("length")
        inv12 = wide("inv12", NEXP + wrap)
        e_len = wide("e_len")
        gsq = carve(NT, NEXP + wrap)
        row_sq = wide("row_sq")
        tmp = wide("tmp")
        tmp2 = wide("tmp2")
        score = wide("score")
        best = wide("best")
        best_at = carve(NT, NEXP).bitcast(U32)
        best_f = wide("best_f")
        places = carve(NEXP)
        pen = carve(4)
        pair = carve(NT, 4)
        roots_done = sem("roots_done")
        row_summed = sem("row_summed")
        row_root = sem("row_root")
        penalty_part = sem("penalty_part")
        penalty_sum = sem("penalty_sum")
        places_set = sem("places_set")
        gap_done = sem("gap_done")
        gap_exp = sem("gap_exp")

        def length_roots():
            nc.scalar.activation(length, dots[:, :, :, 0], ACT.Sqrt)
            nc.scalar.activation(e_len, dots[:, :, :, NSHIFT + 1], ACT.Sqrt).then_inc(roots_done, 1)

        def score_roots(act):
            act.wait_ge(row_summed, 1)
            nc.scalar.activation(tmp, row_sq, ACT.Sqrt).then_inc(row_root, 1)
            act.wait_ge(gap_done, 1)
            nc.scalar.activation(pair[:, :, 1:2], pair[:, :, 0:1], ACT.Exp).then_inc(gap_exp, 1)

        def score_sums(pool):
            nc.gpsimd.iota(places, pattern=[[1, NEXP]], base=0, channel_multiplier=0, allow_small_or_imprecise_dtypes=True).then_inc(places_set, 1)
            pool.wait_ge(penalty_part, 1)
            nc.gpsimd.partition_all_reduce(pen[:, 1:2], pen[:, 0:1], P, RADD).then_inc(penalty_sum, 1)

        def scoring(dve):
            v = nc.vector

            def tt(o, a, b_, op):
                r = v.tensor_tensor(o, a, b_, op)
                dve.drain()
                return r

            def ts(o, a, s1, s2, op0, op1=None):
                r = v.tensor_scalar(o, a, s1, s2, op0, op1) if op1 is not None else v.tensor_scalar(o, a, s1, s2, op0)
                dve.drain()
                return r

            dve.wait_ge(roots_done, 1)
            inv = inv12[:, :, 0:NEXP]
            ts(inv, length, 1e-12, None, ALU.max)
            v.reciprocal(inv, inv)
            dve.drain()
            v.tensor_copy(inv12[:, :, NEXP:], inv12[:, :, 0:wrap])
            dve.drain()
            tt(tmp, dots[:, :, :, 0], inv, ALU.mult)
            tt(tmp, tmp, inv, ALU.mult)
            ts(tmp, tmp, 1.0, None, ALU.subtract)
            tt(row_sq, tmp, tmp, ALU.mult)
            for s in range(1, wrap + 1):
                n = NEXP if s < wrap else wrap
                g = gsq[:, :, wrap:wrap + n]
                tt(g, dots[:, :, 0:n, s], inv12[:, :, 0:n], ALU.mult)
                tt(g, g, inv12[:, :, s:s + n], ALU.mult)
                tt(g, g, g, ALU.mult)
                tt(row_sq[:, :, 0:n], row_sq[:, :, 0:n], g, ALU.add)
                first = min(n, NEXP - s)
                tt(row_sq[:, :, s:s + first], row_sq[:, :, s:s + first], g[:, :, 0:first], ALU.add)
                if first < n:
                    tt(row_sq[:, :, 0:n - first], row_sq[:, :, 0:n - first], g[:, :, first:n], ALU.add)
            dve.drain().then_inc(row_summed, 1)
            dve.wait_ge(row_root, 1)
            ts(tmp, tmp, 1e-12, None, ALU.max)
            v.reciprocal(tmp, tmp)
            dve.drain()
            tt(tmp2, row_sq, tmp, ALU.mult)
            tt(tmp2, tmp2, tmp, ALU.mult)
            v.tensor_reduce(pen[:, 0:1], tmp2.rearrange("p t e -> p (t e)"), axis=AX_X, op=ALU.add).then_inc(penalty_part, 1)
            dve.drain()
            tt(tmp2, length, inv, ALU.mult)
            ts(tmp2, tmp2, 1e-8, None, ALU.max)
            ts(tmp, e_len, 1e-8, None, ALU.max)
            tt(tmp, tmp, tmp2, ALU.mult)
            v.reciprocal(tmp, tmp)
            dve.drain()
            tt(score, dots[:, :, :, NSHIFT], inv, ALU.mult)
            tt(score, score, tmp, ALU.mult)
            ts(score, score, -1.0, 1.0, ALU.mult, ALU.add)
            dve.wait_ge(penalty_sum, 1)
            ts(pen[:, 2:3], pen[:, 1:2], 1.0 / TOK, 1.0, ALU.mult, ALU.add)
            ts(score, score, pen[:, 2:3], None, ALU.mult)
            for n in range(NT):
                v.max(best[:, n, :], score[:, n, :])
            dve.drain()
            for n in range(NT):
                v.max_index(best_at[:, n, :], best[:, n, :], score[:, n, :])
            dve.drain()
            v.tensor_copy(best_f, best_at)
            tt(pair[:, :, 0:1], best[:, :, 1:2], best[:, :, 0:1], ALU.subtract)
            dve.drain().then_inc(gap_done, 1)
            dve.wait_ge(gap_exp, 1)
            dve.wait_ge(places_set, 1)
            ts(pair[:, :, 2:3], pair[:, :, 1:2], 1.0, None, ALU.add)
            v.reciprocal(pair[:, :, 2:3], pair[:, :, 2:3])
            dve.drain()
            tt(pair[:, :, 3:4], pair[:, :, 1:2], pair[:, :, 2:3], ALU.mult)
            every = places.unsqueeze(1).to_broadcast([P, NT, NEXP])
            tt(tmp, every, best_f[:, :, 0:1].to_broadcast([P, NT, NEXP]), ALU.is_equal)
            tt(mix, tmp, pair[:, :, 2:3].to_broadcast([P, NT, NEXP]), ALU.mult)
            tt(tmp, every, best_f[:, :, 1:2].to_broadcast([P, NT, NEXP]), ALU.is_equal)
            tt(tmp, tmp, pair[:, :, 3:4].to_broadcast([P, NT, NEXP]), ALU.mult)
            tt(mix, mix, tmp, ALU.add)

        QT = BANK // P
        RING = 3
        UNITS = NE * FC
        hid_a = [carve(BANK) for _ in range(RING)]
        hid = [carve(BANK) for _ in range(2 * FC)]
        acc = carve(QT, C)
        x2_in = carve(QT, C)
        y_out = carve(QT, C)
        x2t_in = sem("x2t_in")
        gate_ps = sem("gate_ps")
        silu_done = sem("silu_done")
        hid_done = sem("hid_done")
        down_ps = sem("down_ps")
        down_read = sem("down_read")
        f_var = sem("f_var")
        f_std = sem("f_std")
        y_done = sem("y_done")
        y_stored = sem("y_stored")

        def token_rows(dram, tile):
            return dram.rearrange("b t c -> t b c")[bass.ds(tile * SP_T, SP_T)]

        def over_chunks(eng, body):
            body(0, False)
            with eng.Fori(0, NT // QT - 1) as i:
                body(i + 1, True)

        with nc.Block() as block:
            @block.sync
            def _(sp):
                sp.sem_inc(y_done, 1)
                sp.sem_inc(y_stored, 16 * QT)
                with sp.Fori(0, NT // QT) as i:
                    sp.wait_ge(y_done, i + 1)
                    for t in range(QT):
                        sp.dma_start(x2_in[:, t, :], token_rows(x2_dram, i * QT + t)).then_inc(x2t_in, 16)
                    sp.wait_ge(y_done, i + 2)
                    for t in range(QT):
                        sp.dma_start(token_rows(out, i * QT + t), y_out[:, t, :]).then_inc(y_stored, 16)
                sp.wait_ge(y_stored, 16 * NT + 16 * QT)

            @block.tensor
            def _(pe):
                pe.sem_inc(hid_done, RING)
                pe.sem_inc(down_read, 2)
                with pe.Fori(0, NT // QT) as i:
                    toks = xn2T[:, bass.ds(i * BANK, BANK)]

                    def down(e):
                        pe.wait_ge(hid_done, UNITS * i + FC * (e + 1) + RING)
                        pe.wait_ge(down_read, NE * i + e + (2 if e == 0 else 1))
                        for t in range(QT):
                            for f in range(FC):
                                last = nc.tensor.matmul(psum[:, 6 + e % 2, t * P:(t + 1) * P],
                                                        hid[(FC * e + f) % (2 * FC)][:, t * P:(t + 1) * P],
                                                        expT[:, e, 4 + f, :], start=(f == 0), stop=(f == FC - 1))
                        last.then_inc(down_ps, 1)

                    for e in range(NE):
                        for f in range(FC):
                            u = FC * e + f
                            pe.wait_ge(hid_done, UNITS * i + u + 1)
                            for k in range(2):
                                last = nc.tensor.matmul(psum[:, 2 * (u % RING) + k, :], expT[:, e, FC * k + f, :], toks,
                                                        start=True, stop=True)
                            last.then_inc(gate_ps, 1)
                        if e >= 1:
                            down(e - 1)
                    down(NE - 1)

            @block.scalar
            def _(act):
                def roots(n):
                    act.wait_ge(f_var, n)
                    nc.scalar.activation(std[:, 0, :], mv[:, 0, :, 1], ACT.Sqrt, bias=eps[:, 0:1]).then_inc(f_std, 1)

                def chunk(i, follows):
                    for u in range(UNITS):
                        act.wait_ge(gate_ps, UNITS * i + u + 1)
                        act.wait_ge(hid_done, UNITS * i + u + 1)
                        nc.scalar.activation(hid_a[u % RING], psum[:, 2 * (u % RING), :], ACT.Silu).then_inc(silu_done, 1)
                        if follows and u == FC:
                            roots(i)
                        if not follows and u == 2 * FC - 1:
                            score_roots(act)

                length_roots()
                over_chunks(act, chunk)
                roots(NT // QT)

            @block.gpsimd
            def _(pool):
                score_sums(pool)

            @block.vector
            def _(dve):
                def tail_stats():
                    for t in range(QT):
                        nc.vector.bn_stats(stats[:, 0, t, :], acc[:, t, :])
                    dve.drain()
                    for t in range(QT):
                        last = nc.vector.bn_aggr(mv[:, 0, t, :], stats[:, 0, t, :])
                    last.then_inc(f_var, 1)

                def tail_apply(n):
                    dve.wait_ge(f_std, n)
                    nc.vector.reciprocal(rstd[:, 0, :], std[:, 0, :])
                    dve.drain()
                    for t in range(QT):
                        nc.vector.tensor_scalar(acc[:, t, :], acc[:, t, :], mv[:, 0, t, 0:1], rstd[:, 0, t:t + 1], ALU.subtract, ALU.mult)
                    dve.drain()
                    dve.wait_ge(x2t_in, 16 * QT * n)
                    dve.wait_ge(y_stored, 16 * QT * n)
                    nc.vector.tensor_tensor(y_out, acc, x2_in, ALU.add).then_inc(y_done, 1)

                def chunk(i, follows):
                    def collect(e):
                        dve.wait_ge(down_ps, NE * i + e + 1)
                        for t in range(QT):
                            y = psum[:, 6 + e % 2, t * P:(t + 1) * P]
                            if e == 0:
                                w = mix[:, bass.ds(i * QT + t, 1), e:e + 1].rearrange("p a b -> p (a b)")
                                last = nc.vector.tensor_scalar(acc[:, t, :], y, w, None, ALU.mult)
                            elif e < NEXP:
                                w = mix[:, bass.ds(i * QT + t, 1), e:e + 1].rearrange("p a b -> p (a b)")
                                last = nc.vector.scalar_tensor_tensor(acc[:, t, :], y, w, acc[:, t, :], ALU.mult, ALU.add)
                            else:
                                last = nc.vector.tensor_tensor(acc[:, t, :], y, acc[:, t, :], ALU.add)
                        last.then_inc(down_read, 1)
                        dve.drain()

                    for e in range(NE):
                        for f in range(FC):
                            u = FC * e + f
                            dve.wait_ge(silu_done, UNITS * i + u + 1)
                            if e >= 2:
                                dve.wait_ge(down_ps, NE * i + e - 1)
                            nc.vector.tensor_tensor(hid[u % (2 * FC)], hid_a[u % RING], psum[:, 2 * (u % RING) + 1, :], ALU.mult).then_inc(hid_done, 1)
                        if follows and e == 0:
                            tail_stats()
                        if follows and e == 1:
                            tail_apply(i)
                            dve.drain()
                        if not follows and e == 1:
                            scoring(dve)
                        if e >= 1:
                            collect(e - 1)
                    collect(NE - 1)

                over_chunks(dve, chunk)
                tail_stats()
                tail_apply(NT // QT)


_INS = ['L0_attn_x', 'L0_attn_qkv_w', 'L0_attn_qkv_b', 'L0_attn_rpb', 'L0_attn_proj_w', 'L0_attn_proj_b',
        'L0_ffn_gru_w_ih', 'L0_ffn_gru_w_hh', 'L0_ffn_expr_w', 'L0_ffn_ctx_w', 'L0_ffn_ctx_b', 'L0_ffn_gate_w',
        'L0_ffn_up_w', 'L0_ffn_down_w', 'L0_ffn_shared_gate_w', 'L0_ffn_shared_up_w', 'L0_ffn_shared_down_w']
_OUTS = [((8, 512, 128), 'float32')]


def kernel(**inputs):
    import numpy as _np
    import concourse.bacc as _bacc
    from concourse import mybir as _mybir
    from concourse.bass_utils import run_bass_kernel_spmd as _run

    nc = _bacc.Bacc("TRN2", target_bir_lowering=False, num_devices=1)
    arrays, args = {}, []
    for name in _INS:
        a = _np.ascontiguousarray(inputs[name])
        arrays[f"in_{name}_dram"] = a
        args.append(nc.dram_tensor(f"in_{name}_dram", a.shape, _mybir.dt.from_np(a.dtype), kind="ExternalInput").ap())
    for i, (shape, dtype) in enumerate(_OUTS):
        dt = _mybir.dt.from_np(_np.dtype(dtype))
        args.append(nc.dram_tensor(f"out_{i}_dram", shape, dt, kind="ExternalOutput").ap())
    sandwich(nc, *args)
    r = _run(nc, [arrays], core_ids=[0])
    got = tuple(r.results[0][f"out_{i}_dram"] for i in range(len(_OUTS)))
    return got[0]
```
